# Optimizing a Trainium2 kernel written in Bass

```python
import numpy as np
import jax
import jax.numpy as jnp

def _softmax(x, axis=-1):
    return jax.nn.softmax(x, axis=axis)

def _gelu(x):
    return jax.nn.gelu(x, approximate=True)

def _silu(x):
    return jax.nn.silu(x)

def _sigmoid(x):
    return jax.nn.sigmoid(x)

def _layernorm(x, axis=-1, eps=1e-05):
    m = jnp.mean(x, axis=axis, keepdims=True)
    v = jnp.var(x, axis=axis, keepdims=True)
    return (x - m) / jnp.sqrt(v + eps)

def _scatter_add(tgt, idx, src, axis=0):
    return tgt.at[idx].add(src)

def _segment_sum(src, seg, n):
    return jax.ops.segment_sum(src, seg, n)
kernel_name = 'mk_gnn_resnorm_d1_gnn_r32_9b999e'

def setup_inputs(seed: int=0):
    np.random.seed(seed)
    _w = jnp.asarray

    def _rec_inputs():
        import jax
        import jax.numpy as jnp
        _gk = jax.random.key(seed)
        x = -8.776e-05 + 1 * jax.random.normal(jax.random.fold_in(_gk, 1), (50000, 512), jnp.float32)
        src = jax.random.randint(jax.random.fold_in(_gk, 2), (25000,), 0, 50000, jnp.int32)
        dst = jnp.minimum((50000 * jax.random.uniform(jax.random.fold_in(_gk, 3), (25000,)) ** 2.0).astype(jnp.int32), 49999)
        _o = jnp.argsort(dst, stable=True)
        src = src[_o]
        dst = dst[_o]
        return (x, src, dst)
    x, src, dst = _rec_inputs()

    def _L0_gnn_setup():
        import jax, jax.numpy as jnp
        import numpy as np
        N_NODES = 10000
        N_EDGES = 5000
        D = 512
        key = jax.random.key(seed)
        k_h, k_e, k_w1, k_w2 = jax.random.split(key, 4)
        h = jax.random.normal(k_h, (N_NODES, D), dtype=jnp.float32)
        edge_index = jax.random.randint(k_e, (2, N_EDGES), 0, N_NODES, dtype=jnp.int64)
        scale = 1.0 / np.sqrt(D)
        W1 = jax.random.normal(k_w1, (D, D), dtype=jnp.float32) * scale
        b1 = jnp.zeros((D,), dtype=jnp.float32)
        W2 = jax.random.normal(k_w2, (D, D), dtype=jnp.float32) * scale
        b2 = jnp.zeros((D,), dtype=jnp.float32)
        return {'h': h, 'edge_index': edge_index, 'W1': W1, 'b1': b1, 'W2': W2, 'b2': b2}
    _L0_gnn_all = _L0_gnn_setup()
    _L0_gnn_in = {k: v for k, v in _L0_gnn_all.items() if k in ('W1', 'b1', 'W2', 'b2')}
    del _L0_gnn_all
    return {'x': x, 'src': src, 'dst': dst, 'L0_gnn_W1': _L0_gnn_in['W1'], 'L0_gnn_b1': _L0_gnn_in['b1'], 'L0_gnn_W2': _L0_gnn_in['W2'], 'L0_gnn_b2': _L0_gnn_in['b2']}

def reference(x, src, dst, L0_gnn_W1, L0_gnn_b1, L0_gnn_W2, L0_gnn_b2):
    import jax
    import jax.numpy as jnp

    def _L0_gnn_ref(h, edge_index, W1, b1, W2, b2):
        import jax, jax.numpy as jnp
        import numpy as np
        N_NODES = 10000
        N_EDGES = 5000
        D = 512
        send, rec = (edge_index[0], edge_index[1])
        agg = jax.ops.segment_sum(h[send], rec, num_segments=h.shape[0])
        x = h + agg
        x = jax.nn.relu(x @ W1 + b1)
        x = x @ W2 + b2
        return x
    edge_index = jnp.stack([src, dst])
    x = _layernorm(x + _L0_gnn_ref(x, edge_index, L0_gnn_W1, L0_gnn_b1, L0_gnn_W2, L0_gnn_b2), axis=-1)
    return x

_drawn_inputs = setup_inputs


def setup_inputs(seed=0):
    import zlib

    import numpy as np

    out = dict(_drawn_inputs(seed))
    spreads = {'L0_gnn_b1': (0.0, 0.1), 'L0_gnn_b2': (0.0, 0.1)}
    factors = {}
    for name, (base, spread) in spreads.items():
        noise = np.random.default_rng([zlib.crc32(name.encode()), seed]).standard_normal(out[name].shape)
        drawn = base * np.exp(spread * noise) if base else spread * noise
        out[name] = jnp.asarray(drawn.astype(out[name].dtype))
    for name, factor in factors.items():
        out[name] = (out[name] * factor).astype(out[name].dtype)
    return out
```

```python
from contextlib import ExitStack

import concourse.bass as bass
from concourse import mybir

ALU = mybir.AluOpType
ACT = mybir.ActivationFunctionType
F32 = mybir.dt.float32
F32R = mybir.dt.float32r
I32 = mybir.dt.int32
U32 = mybir.dt.uint32
AX_X = mybir.AxisListType.X

P = 128
TPG = 4
EPS = 1e-5


def gnn_layer_with_residual_norm(nc, x, src, dst, w1, b1, w2, b2, out):
    n_nodes, d = x.shape
    n_edges = src.shape[0]
    kb_n = d // P
    gw = TPG * P
    last = n_nodes // gw
    last_tiles = -(-(n_nodes - last * gw) // P)
    last_base = n_nodes - last_tiles * P
    last_skip = last * gw - last_base
    n_tiles = last * TPG + last_tiles
    assert d == gw and 0 < last_tiles < TPG and 0 <= last_skip < P and last < P
    er = 125
    ec = n_edges // er
    assert er * ec == n_edges
    step_edges = 2 * P
    step_bits = step_edges.bit_length() - 1
    pad_edges = 4 * P
    max_steps = n_edges // step_edges + 1
    first_looped = 2
    n_pairs = (last - 3 - first_looped + 1) // 2
    after_loop = first_looped + 2 * n_pairs
    assert n_pairs >= 1

    edge_pairs = nc.dram_tensor("edge_pairs", (n_edges + step_edges * (max_steps + 2), 2), U32, kind="Internal").ap()
    tile_table = nc.dram_tensor("tile_table", (P * TPG * 4,), I32, kind="Internal").ap()

    ctx = ExitStack()
    with ctx:
        def sb(name, shape, dt):
            return ctx.enter_context(nc.sbuf_tensor(name, shape, dt))

        def sem(name):
            return ctx.enter_context(nc.semaphore(name))

        def sems(name, n):
            return [sem(f"{name}{i}") for i in range(n)]

        w_stage = sb("w_stage", [P, kb_n, d], F32)
        w1_hi, w1_lo = sb("w1_hi", [P, kb_n, d], F32R), sb("w1_lo", [P, kb_n, d], F32R)
        w2_hi, w2_lo = sb("w2_hi", [P, kb_n, d], F32R), sb("w2_lo", [P, kb_n, d], F32R)
        b1_col = sb("b1_col", [P, kb_n], F32)
        b2_rows = sb("b2_rows", [P, d], F32)
        x_rows = [[sb(f"x_rows{a}{i}", [P, d], F32) for i in range(TPG)] for a in range(2)]
        xb_mem = sb("xb_mem", [P, 2 * TPG * d], F32)
        xb_rows = [[xb_mem[:, (TPG * a + i) * d:(TPG * a + i + 1) * d] for i in range(TPG)] for a in range(2)]
        h_rows = [sb(f"h_rows{i}", [P, d], F32) for i in range(2)]
        ht_hi = [sb(f"ht_hi{a}", [P, kb_n, gw], F32R) for a in range(2)]
        ht_lo = [sb(f"ht_lo{a}", [P, kb_n, gw], F32R) for a in range(2)]
        relu_f = [sb(f"relu_f{i}", [P, gw], F32) for i in range(2)]
        r_hi = [sb(f"r_hi{a}", [P, kb_n, gw], F32R) for a in range(2)]
        r_lo = [sb(f"r_lo{a}", [P, kb_n, gw], F32R) for a in range(2)]
        edges_in = [sb(f"edges_in{i}", [P, 2], U32) for i in range(TPG)]
        nbr = [sb(f"nbr{i}", [P, d], F32) for i in range(TPG)]
        nbr_hi = [sb(f"nbr_hi{i}", [P, d], F32R) for i in range(2)]
        nbr_lo = [sb(f"nbr_lo{i}", [P, d], F32R) for i in range(2)]
        onehot = [sb(f"onehot{i}", [P, P], F32R) for i in range(2)]
        more_in = [sb(f"more_in{a}", [P, 2], U32) for a in range(2)]
        more_base = [sb(f"more_base{i}", [P, 1], F32) for i in range(TPG)]
        more_nbr = [sb(f"more_nbr{a}", [P, d], F32) for a in range(2)]
        more_onehot = [sb(f"more_onehot{a}", [P, P], F32) for a in range(2)]
        y_mem, o_mem = sb("y_mem", [P, TPG * d], F32), sb("o_mem", [P, TPG * d], F32)
        y_rows = [y_mem[:, i * d:(i + 1) * d] for i in range(TPG)]
        o_rows = [o_mem[:, i * d:(i + 1) * d] for i in range(TPG)]
        bn_parts = [sb(f"bn_parts{i}", [P, 6], F32) for i in range(TPG)]
        mean_var = [sb(f"mean_var{i}", [P, 2], F32) for i in range(TPG)]
        std = [sb(f"std{i}", [P, 1], F32) for i in range(TPG)]
        rstd = [sb(f"rstd{i}", [P, 1], F32) for i in range(TPG)]
        neg_mean = [sb(f"neg_mean{i}", [P, 1], F32) for i in range(TPG)]
        eps_col = sb("eps_col", [P, 1], F32)
        base_of = sb("base_of", [P, n_tiles], F32)
        iota_i = sb("iota_i", [P, n_tiles], I32)
        iota_f = sb("iota_f", [P, P], F32)
        iota_p_i, iota_p = sb("iota_p_i", [P, 1], I32), sb("iota_p", [P, 1], F32)
        ident = sb("ident", [P, P], F32)
        below = sb("below", [P, P], F32)
        ones = sb("ones", [P, P], F32)
        dst_i, src_i = sb("dst_i", [er, ec], I32), sb("src_i", [er, ec], I32)
        dst_next = sb("dst_next", [er, ec], I32)
        drops = sb("drops", [er, ec], F32)
        drops_sum = sb("drops_sum", [er, 1], F32)
        unsorted_i = sb("unsorted_i", [1, 1], I32)
        pair_rows = sb("pair_rows", [er, ec, 2], U32)
        pad_rows = sb("pad_rows", [P, pad_edges // P, 2], U32)
        row_first = sb("row_first", [er, 2], U32)
        first_diag = sb("first_diag", [er, er], F32)
        bound_i, bound = sb("bound_i", [P, 2 * TPG], I32), sb("bound", [P, 2 * TPG], F32)
        last_shift = sb("last_shift", [P, 1], F32)
        rows_below = o_mem[:, 0:2 * TPG * er].rearrange("p (c r) -> p c r", r=er)
        row_no, row_no_i = sb("row_no", [P, 2 * TPG], F32), sb("row_no_i", [P, 2 * TPG], U32)
        cut_row = [xb_mem[:, 2 * ec * c:2 * ec * (c + 1)].bitcast(U32) for c in range(2 * TPG)]
        edges_below = y_mem[:, 0:2 * TPG * ec].rearrange("p (c r) -> p c r", r=ec)
        edges_no = sb("edges_no", [P, 2 * TPG], F32)
        sort_w, sort_parts = 5 * ec, er // 5
        own_no, own_dst2 = sb("own_no", [er, ec], F32), sb("own_dst2", [er, ec], F32)
        place, place_part = sb("place", [er, ec], F32), sb("place_part", [er, 1], F32)
        other_i, other_dst2, is_before, goes_before = (xb_mem[0:er, n * sort_w:(n + 1) * sort_w] for n in range(4))
        other_i = other_i.bitcast(I32)
        local_no, local_no_i = y_mem[0:er, 0:sort_w], y_mem[0:er, sort_w:2 * sort_w].bitcast(I32)
        own_no_i = sb("own_no_i", [er, ec], I32)
        pair_col, place_col = sb("pair_col", [er, 2], U32), sb("place_col", [er, 1], U32)
        extra, extra_i = sb("extra", [P, TPG], F32), sb("extra_i", [P, TPG], I32)
        steps_before = sb("steps_before", [P, TPG + 1], F32)
        tile_info = sb("tile_info", [P, TPG, 4], I32)
        tile_row = sb("tile_row", [1, P * TPG * 4], I32)

        banks = [ctx.enter_context(nc.psum_tensor(f"bank{i}", [P, d], F32)) for i in range(8)]
        agg_ps, ht_ps, l1_ps, l2_ps = banks[0:2], banks[2:4], banks[4:6], banks[6:8]

        w_in = sems("w_in", 2)
        consts_in = sem("consts_in")
        eps_set = sem("eps_set")
        w_hi_done, w_lo_done = sem("w_hi_done"), sem("w_lo_done")
        iotas_done = sem("iotas_done")
        step_dve = sem("step_dve")
        edges_loaded = sem("edges_loaded")
        next_cleared, next_loaded = sem("next_cleared"), sem("next_loaded")
        pairs_made, pairs_stored = sem("pairs_made"), sem("pairs_stored")
        drops_done, drops_counted = sem("drops_done"), sem("drops_counted")
        flag_made = sem("flag_made")
        order_final = sem("order_final")
        firsts_in, diag_made, firsts_spread = sem("firsts_in"), sem("diag_made"), sem("firsts_spread")
        rows_known, cut_rows_in = sem("rows_known"), sems("cut_rows_in", 2 * TPG)
        totals_made, totals_spread = sem("totals_made"), sem("totals_spread")
        info_made, info_stored, table_in = sem("info_made"), sem("info_stored"), sem("table_in")
        x_in = [sems(f"x_in{a}", TPG) for a in range(2)]
        edges_in_done = sems("edges_in_done", TPG)
        nbr_in = sems("nbr_in", TPG)
        nbr_hi_done, nbr_lo_done, onehot_done = sem("nbr_hi_done"), sem("nbr_lo_done"), sem("onehot_done")
        agg_done, h_done, ht_done = sem("agg_done"), sem("h_done"), sem("ht_done")
        ht_hi_done, ht_lo_done = sem("ht_hi_done"), sem("ht_lo_done")
        l1_done, relu_done = sem("l1_done"), sem("relu_done")
        r_hi_done, r_lo_done = sem("r_hi_done"), sem("r_lo_done")
        l2_done, xb_done, y_done = sem("l2_done"), sem("xb_done"), sem("y_done")
        bn_done, stats_done, std_done = sem("bn_done"), sem("stats_done"), sem("std_done")
        rstd_done, neg_mean_done = sem("rstd_done"), sem("neg_mean_done")
        norm_done = sem("norm_done")
        stored = sems("stored", TPG)
        more_edges_in = sems("more_edges_in", 2)
        more_base_done = sem("more_base_done")
        more_nbr_in = sems("more_nbr_in", 2)
        more_onehot_done = sems("more_onehot_done", 2)
        more_used = sems("more_used", 2)
        sort_step = sem("sort_step")
        sort_part_used, sort_part_in = sem("sort_part_used"), sem("sort_part_in")
        places_known, sort_column, sort_put = sem("places_known"), sem("sort_column"), sem("sort_put")

        base_of_made = 3

        block = ctx.enter_context(nc.Block())

        def plus(group, c):
            return group[0], group[1] + c

        def number(group):
            return 2 * group[0] + group[1]

        def visits(group):
            return group[0] + group[1] // 2 + 1

        def tile_of(group, i):
            return plus(group, i // TPG), i % TPG

        def looped(group):
            return not isinstance(group[0], int)

        def is_last(group):
            return not looped(group) and group[1] == last

        def exists(tile):
            group, i = tile
            return looped(group) or 0 <= group[1] < last or (group[1] == last and i < last_tiles)

        def group_exists(group):
            return looped(group) or 0 <= group[1] <= last

        def tile_no(tile):
            group, i = tile
            return 2 * TPG * group[0] + TPG * group[1] + i

        def count(tile):
            return tile_no(tile) + 1

        def width(group):
            return last_tiles * P if is_last(group) else gw

        def rows_of(tile):
            group, i = tile
            if is_last(group):
                return bass.ds(last_base + i * P, P)
            return bass.ds(2 * gw * group[0] + gw * group[1] + i * P, P)

        def wait(eng, semaphore, value):
            if isinstance(value, int) and value <= 0:
                return
            eng.wait_ge(semaphore, value)

        def wait_apart(eng, *waits):
            for _, value in waits:
                eng.compute_val(value)
            eng.wait_ge(flag_made, 1)
            for semaphore, value in waits:
                wait(eng, semaphore, value)

        def over_groups(eng, body):
            for c in range(-1, first_looped):
                body((0, c))
            with eng.Fori(0, n_pairs) as m:
                body((m, first_looped))
                body((m, first_looped + 1))
            for c in range(after_loop, last + 2):
                body((0, c))

        def first_of(eng, tile):
            return eng.value_load(tile_row[0:1, bass.ds(4 * tile_no(tile), 1)], min_val=0, max_val=n_edges)

        def steps_of(eng, tile):
            return eng.value_load(tile_row[0:1, bass.ds(4 * tile_no(tile) + 1, 1)], min_val=0, max_val=max_steps)

        def before_of(eng, tile):
            return eng.value_load(tile_row[0:1, bass.ds(4 * tile_no(tile) + 2, 1)], min_val=1,
                                  max_val=max_steps + n_tiles)

        @block.sync
        def _(sp):
            sp.dma_start(dst_i[:], dst.rearrange("(r c) -> r c", c=ec)).then_inc(edges_loaded, 16)
            sp.dma_start(src_i[:], src.rearrange("(r c) -> r c", c=ec)).then_inc(edges_loaded, 16)
            sp.wait_ge(next_cleared, 1)
            sp.dma_start(dst_next[0:er - 1, :], dst[1:1 + (er - 1) * ec].rearrange("(r c) -> r c", c=ec)
                         ).then_inc(next_loaded, 16)
            sp.dma_start(dst_next[er - 1:er, 0:ec - 1], dst[(er - 1) * ec + 1:n_edges].rearrange("(r c) -> r c", r=1)
                         ).then_inc(next_loaded, 16)
            sp.wait_ge(pairs_made, 1)
            sp.dma_start(edge_pairs[0:n_edges, :].rearrange("(r c) t -> r c t", c=ec), pair_rows[:]
                         ).then_inc(pairs_stored, 16)
            sp.dma_start(edge_pairs[n_edges:n_edges + pad_edges, :].rearrange("(r c) t -> r c t", r=P), pad_rows[:]
                         ).then_inc(pairs_stored, 16)
            for i in range(TPG):
                sp.dma_start(x_rows[0][i][:], x[rows_of(((0, 0), i)), :]).then_inc(x_in[0][i], 16)
            sp.wait_ge(order_final, 1)
            sp.dma_start(row_first[:], edge_pairs[0:n_edges, :].rearrange("(r c) t -> r c t", c=ec)[:, 0, :]
                         ).then_inc(firsts_in, 16)
            sp.wait_ge(info_made, 1)
            sp.dma_start(tile_table.rearrange("(p c) -> p c", p=P), tile_info[:].rearrange("p t c -> p (t c)")
                         ).then_inc(info_stored, 16)
            sp.wait_ge(info_stored, 16)
            sp.dma_start(tile_row[:], tile_table.rearrange("(o c) -> o c", o=1)).then_inc(table_in, 16)
            sp.wait_ge(table_in, 16)

            def load_edges(tile, first):
                sp.dma_start(edges_in[tile[1]][:], edge_pairs[bass.ds(first, P), :]
                             ).then_inc(edges_in_done[tile[1]], 16)

            for i in range(TPG):
                load_edges(((0, 0), i), first_of(sp, ((0, 0), i)))

            def group_loads(group):
                for i in range(TPG):
                    ahead = tile_of(plus(group, 2), i)
                    if exists(ahead):
                        first = first_of(sp, ahead)
                        wait(sp, onehot_done, count(ahead) - TPG)
                        wait(sp, nbr_in[i], 16 * number(ahead[0]))
                        load_edges(ahead, first)
                    tile = tile_of(plus(group, 1), i)
                    if exists(tile):
                        steps = steps_of(sp, tile)
                        with sp.If(steps > 0):
                            first, before = first_of(sp, tile), before_of(sp, tile)
                            with sp.Fori(0, steps) as k:
                                for a in range(2):
                                    wait_apart(sp, (more_onehot_done[a], before + k),
                                               (more_nbr_in[a], 16 * (before + k)))
                                    at = first + step_edges * k + P * (a + 1)
                                    sp.dma_start(more_in[a][:], edge_pairs[bass.ds(at, P), :]).then_inc(more_edges_in[a], 16)
                            sp.nop()
                    if exists(ahead):
                        a = ahead[0][1] % 2
                        wait(sp, xb_done, count(tile_of(group, i)))
                        sp.dma_start(x_rows[a][i][:], x[rows_of(ahead), :]).then_inc(x_in[a][i], 16)

            over_groups(sp, group_loads)

        @block.gpsimd
        def _(pool):
            nc.gpsimd.iota(iota_i[:], pattern=[[P, n_tiles]], base=0, channel_multiplier=0).then_inc(iotas_done, 1)
            nc.gpsimd.iota(iota_p_i[:], pattern=[[0, 1]], base=0, channel_multiplier=1).then_inc(iotas_done, 1)
            nc.gpsimd.iota(bound_i[:], pattern=[[P, 2], [P, TPG]], base=0, channel_multiplier=gw
                           ).then_inc(iotas_done, 1)
            nc.gpsimd.iota(iota_f[:], pattern=[[1, P]], base=0, channel_multiplier=0,
                           allow_small_or_imprecise_dtypes=True).then_inc(iotas_done, 1)

            def put_sorted():
                with pool.Fori(0, sort_parts) as q:
                    wait_apart(pool, (sort_part_used, q + 1))
                    pool.dma_start(other_i, dst[bass.ds(q * sort_w, sort_w)].rearrange("(o c) -> o c", o=1)
                                   .to_broadcast([er, sort_w])).then_inc(sort_part_in, 16)
                pool.wait_ge(places_known, 1)
                with pool.Fori(0, ec) as j:
                    nc.gpsimd.tensor_copy(pair_col[:], pair_rows[:, bass.ds(j, 1), :].rearrange("p o t -> p (o t)"))
                    nc.gpsimd.tensor_copy(place_col[:], place[:, bass.ds(j, 1)]).then_inc(sort_column, 1)
                    wait_apart(pool, (sort_column, j + 1))
                    pool.indirect_dma_start(edge_pairs, bass.IndirectOffsetOnAxis(ap=place_col[:], axis=0),
                                            pair_col[:], None).then_inc(sort_put, 16)
                    pool.wait_ge(sort_put, 16 * (j + 1))

            nc.gpsimd.iota(own_no_i[:], pattern=[[1, ec]], base=0, channel_multiplier=ec).then_inc(iotas_done, 1)
            nc.gpsimd.iota(local_no_i, pattern=[[1, sort_w]], base=0, channel_multiplier=0).then_inc(iotas_done, 1)
            for a in range(2):
                pool.dma_start(more_nbr[a][:], x[0:P, :]).then_inc(more_nbr_in[a], 16)
                nc.gpsimd.memset(more_onehot[a][:], 0.0).then_inc(more_onehot_done[a], 1)
            pool.wait_ge(flag_made, 1)
            pool.wait_ge(pairs_stored, 32)
            unsorted = pool.value_load(unsorted_i[:], min_val=0, max_val=n_edges)
            with pool.If(unsorted > 0):
                put_sorted()
                pool.nop()
            nc.gpsimd.memset(more_base[0][:], 0.0).then_inc(order_final, 1)
            pool.wait_ge(rows_known, 1)
            edge_rows = edge_pairs[0:n_edges, :].rearrange("(r c) t -> r (c t)", c=ec)
            for c in range(2 * TPG):
                pool.indirect_dma_start(cut_row[c], None, edge_rows,
                                        bass.IndirectOffsetOnAxis(ap=row_no_i[:, c:c + 1], axis=0)
                                        ).then_inc(cut_rows_in[c], 16)

            def gather(tile):
                i = tile[1]
                wait_apart(pool, (edges_in_done[i], 16 * (number(tile[0]) + 1)),
                           (nbr_hi_done, count(tile) - TPG), (nbr_lo_done, count(tile) - TPG))
                pool.indirect_dma_start(nbr[i][:], None, x,
                                        bass.IndirectOffsetOnAxis(ap=edges_in[i][:, 0:1], axis=0)
                                        ).then_inc(nbr_in[i], 16)

            def split_lo(tile):
                i = tile[1]
                pool.wait_ge(nbr_hi_done, count(tile))
                wait(pool, agg_done, count(tile) - 2)
                nc.gpsimd.tensor_tensor(nbr_lo[i % 2][:], nbr[i][:], nbr_hi[i % 2][:].bitcast(F32), ALU.subtract
                                        ).then_inc(nbr_lo_done, 1)

            def further_steps(tile):
                steps = steps_of(pool, tile)
                nc.gpsimd.tensor_copy(more_base[tile[1]][:], base_of[:, bass.ds(tile_no(tile), 1)]
                                      ).then_inc(more_base_done, 1)
                with pool.If(steps > 0):
                    before = before_of(pool, tile)
                    wait_apart(pool, (more_base_done, count(tile)))
                    with pool.Fori(0, steps) as k:
                        for a in range(2):
                            wait_apart(pool, (more_edges_in[a], 16 * (before + k)), (more_used[a], before + k))
                            pool.indirect_dma_start(more_nbr[a][:], None, x,
                                                    bass.IndirectOffsetOnAxis(ap=more_in[a][:, 0:1], axis=0)
                                                    ).then_inc(more_nbr_in[a], 16)
                            nc.gpsimd.tensor_scalar(more_onehot[a][:], iota_f[:], more_base[tile[1]][:],
                                                    more_in[a][:, 1:2].bitcast(F32), ALU.add, ALU.is_equal
                                                    ).then_inc(more_onehot_done[a], 1)
                    pool.nop()

            pool.wait_ge(table_in, 16)
            pool.wait_ge(step_dve, base_of_made)
            for i in range(TPG - 1):
                gather(((0, 0), i))
            split_lo(((0, 0), 0))
            pool.wait_ge(consts_in, 32)

            def group_edges(group):
                for i in range(TPG):
                    for tile, work in ((tile_of(plus(group, 1), i + 3), gather),
                                       (tile_of(plus(group, 1), i + 1), split_lo),
                                       (tile_of(plus(group, 1), i), further_steps)):
                        if exists(tile):
                            work(tile)
                    tile = tile_of(group, i)
                    if exists(tile):
                        a = group[1] % 2
                        pool.wait_ge(x_in[a][i], 16 * visits(group))
                        pool.wait_ge(h_done, count(tile))
                        wait(pool, y_done, count(tile) - 2 * TPG)
                        nc.gpsimd.tensor_tensor(xb_rows[a][i], x_rows[a][i][:], b2_rows[:], ALU.add
                                                ).then_inc(xb_done, 1)

            over_groups(pool, group_edges)

        @block.scalar
        def _(act):
            act.dma_start(w_stage[:], w1.rearrange("(k p) n -> p k n", p=P)).then_inc(w_in[0], 16)
            act.dma_start(b1_col[:], b1.rearrange("(k p) -> p k", p=P),
                          allow_slow_non_contiguous=True).then_inc(consts_in, 16)
            act.dma_start(b2_rows[:], b2.rearrange("(o n) -> o n", o=1).to_broadcast([P, d])
                          ).then_inc(consts_in, 16)
            for n, (hi, w) in enumerate(((w1_hi, w2), (w2_hi, None))):
                act.wait_ge(w_in[n], 16)
                nc.scalar.copy(hi[:], w_stage[:]).then_inc(w_hi_done, 1)
                if w is not None:
                    act.wait_ge(w_lo_done, 1)
                    act.dma_start(w_stage[:], w.rearrange("(k p) n -> p k n", p=P)).then_inc(w_in[1], 16)
            act.wait_ge(consts_in, 32)
            act.wait_ge(eps_set, 1)

            def split_hi(tile):
                i = tile[1]
                act.wait_ge(nbr_in[i], 16 * (number(tile[0]) + 1))
                wait(act, agg_done, count(tile) - 2)
                nc.scalar.copy(nbr_hi[i % 2][:], nbr[i][:]).then_inc(nbr_hi_done, 1)

            split_hi(((0, 0), 0))

            def group_act(group):
                for i in range(TPG):
                    half = group[1] % 2
                    n = width(group) if group_exists(group) else 0
                    block_no = count((group, i))
                    tile = tile_of(plus(group, 1), i + 1)
                    if exists(tile):
                        split_hi(tile)
                    if group_exists(group):
                        act.wait_ge(l1_done, block_no)
                        wait(act, r_lo_done, block_no - 2)
                        nc.scalar.activation(relu_f[i % 2][:, 0:n], l1_ps[i % 2][:, 0:n], ACT.Relu,
                                             bias=b1_col[:, i:i + 1]).then_inc(relu_done, 1)
                    tile = tile_of(plus(group, 1), i)
                    if exists(tile):
                        act.wait_ge(ht_done, count(tile))
                        nc.scalar.copy(ht_hi[1 - half][:, :, i * P:(i + 1) * P],
                                       ht_ps[i % 2][:].rearrange("p (k n) -> p k n", n=P)).then_inc(ht_hi_done, 1)
                    if group_exists(group):
                        act.wait_ge(relu_done, block_no)
                        wait(act, l2_done, count((plus(group, -2), TPG - 1)))
                        nc.scalar.copy(r_hi[half][:, i, 0:n], relu_f[i % 2][:, 0:n]).then_inc(r_hi_done, 1)
                    tile = tile_of(plus(group, -1), i - 2)
                    if exists(tile):
                        normalise(tile)
                    tile = tile_of(plus(group, -1), i - 1)
                    if exists(tile):
                        act.wait_ge(stats_done, count(tile))
                        nc.scalar.activation(std[tile[1]][:], mean_var[tile[1]][:, 1:2], ACT.Sqrt,
                                             bias=eps_col[:]).then_inc(std_done, 1)

            def normalise(tile):
                group, i = tile
                act.wait_ge(neg_mean_done, count(tile))
                wait(act, stored[i], 16 * number(group))
                nc.scalar.activation(o_rows[i], y_rows[i], ACT.Identity, bias=neg_mean[i][:],
                                     scale=rstd[i][:]).then_inc(norm_done, 1)
                act.wait_ge(norm_done, count(tile))
                if is_last(group) and i == 0:
                    if last_skip < P:
                        act.dma_start(out[last * gw:last_base + P, :], o_rows[i][last_skip:P, :]
                                      ).then_inc(stored[i], 16)
                else:
                    act.dma_start(out[rows_of(tile), :], o_rows[i]).then_inc(stored[i], 16)

            over_groups(act, group_act)
            for tile in (tile_of((0, last + 1), i - 2) for i in range(TPG)):
                if exists(tile):
                    normalise(tile)
            for i in range(TPG):
                act.wait_ge(stored[i], 16 * (last + (1 if i < last_tiles else 0)))

        @block.vector
        def _(dve):
            chain = [0]

            def then(instruction):
                chain[0] += 1
                instruction.then_inc(step_dve, 1)
                dve.wait_ge(step_dve, chain[0])

            V = nc.vector
            V.memset(dst_next[:], 1 << 24).then_inc(next_cleared, 1)
            V.memset(eps_col[:], EPS).then_inc(eps_set, 1)
            V.memset(pad_rows[:, :, 0], 0)
            V.memset(pad_rows[:, :, 1].bitcast(F32), -1.0)
            then(V.memset(ones[:], 1.0))
            dve.wait_ge(iotas_done, 4)
            V.tensor_copy(bound[:], bound_i[:])
            V.tensor_copy(base_of[:], iota_i[:])
            then(V.tensor_copy(iota_p[:], iota_p_i[:]))
            V.tensor_scalar(ident[:], iota_f[:], iota_p[:], None, ALU.is_equal)
            V.tensor_scalar(below[:], iota_f[:], iota_p[:], None, ALU.is_gt)
            V.tensor_scalar(last_shift[:], iota_p[:], float(last), -float(last_skip), ALU.is_equal, ALU.mult)
            then(V.tensor_scalar(base_of[:, last * TPG:], base_of[:, last * TPG:], float(last_skip), None,
                                 ALU.subtract))
            assert chain[0] == base_of_made
            then(V.tensor_scalar(bound[:], bound[:], last_shift[:], None, ALU.add))

            dve.wait_ge(edges_loaded, 32)
            V.tensor_copy(pair_rows[:, :, 0], src_i[:])
            V.tensor_copy(pair_rows[:, :, 1].bitcast(F32), dst_i[:]).then_inc(pairs_made, 1)
            dve.wait_ge(next_loaded, 32)
            then(V.tensor_tensor(drops[:], dst_next[:], dst_i[:], ALU.is_lt))
            V.tensor_reduce(drops_sum[:], drops[:], AX_X, ALU.add).then_inc(drops_done, 1)
            dve.wait_ge(drops_counted, 1)
            V.tensor_copy(unsorted_i[:], banks[0][0:1, 0:1]).then_inc(flag_made, 1)

            def split_weights(n, hi, lo):
                dve.wait_ge(w_hi_done, n + 1)
                V.tensor_tensor(lo[:], w_stage[:], hi[:].bitcast(F32), ALU.subtract).then_inc(w_lo_done, 1)

            split_weights(0, w1_hi, w1_lo)
            def find_places():
                per_column, per_part = 4, 2

                def step(instruction, value):
                    instruction.then_inc(sort_step, 1)
                    dve.wait_ge(sort_step, value)

                V.tensor_copy(own_no[:], own_no_i[:])
                V.tensor_copy(local_no, local_no_i)
                V.memset(place[:], 0.0)
                step(V.tensor_scalar(own_dst2[:], dst_i[:], 2.0, None, ALU.mult), 1)
                V.memset(place_part[:], 0.0).then_inc(sort_part_used, 1)
                with dve.Fori(0, sort_parts) as q:
                    at_part = 1 + q * (per_part + per_column * ec)
                    dve.wait_ge(sort_part_in, 16 * (q + 1))
                    V.tensor_scalar(other_dst2, other_i, 2.0, None, ALU.mult).then_inc(sort_step, 1)
                    wait_apart(dve, (sort_step, at_part + 1))
                    with dve.Fori(0, ec) as j:
                        at = at_part + 1 + per_column * j
                        step(V.tensor_scalar(is_before, local_no, own_no[:, bass.ds(j, 1)], None, ALU.is_lt),
                             at + 1)
                        step(V.scalar_tensor_tensor(out=goes_before, in0=other_dst2,
                                                    scalar=own_dst2[:, bass.ds(j, 1)], in1=is_before,
                                                    op0=ALU.subtract, op1=ALU.is_lt), at + 2)
                        step(V.tensor_reduce(place_part[:], goes_before, AX_X, ALU.add), at + 3)
                        step(V.tensor_tensor(place[:, bass.ds(j, 1)], place[:, bass.ds(j, 1)], place_part[:],
                                             ALU.add), at + 4)
                    step(V.tensor_scalar(own_no[:], own_no[:], float(sort_w), None, ALU.subtract),
                         at_part + 2 + per_column * ec)
                    V.memset(place_part[:], 0.0).then_inc(sort_part_used, 1)
                V.memset(place_part[:], 0.0).then_inc(places_known, 1)

            dve.wait_ge(flag_made, 1)
            unsorted = dve.value_load(unsorted_i[:], min_val=0, max_val=n_edges)
            with dve.If(unsorted > 0):
                dve.wait_ge(iotas_done, 6)
                find_places()
                dve.nop()

            dve.wait_ge(firsts_in, 16)
            V.tensor_scalar(first_diag[:], ident[0:er, 0:er], row_first[:, 1:2].bitcast(F32), None, ALU.mult
                            ).then_inc(diag_made, 1)
            dve.wait_ge(firsts_spread, 1)
            for c in range(2 * TPG):
                ins = V.tensor_scalar(rows_below[:, c, :], banks[1][:, 0:er], bound[:, c:c + 1], None, ALU.is_lt)
            then(ins)
            then(V.tensor_reduce(row_no[:], rows_below, AX_X, ALU.add))
            then(V.tensor_scalar(row_no[:], row_no[:], 1.0, 0.0, ALU.subtract, ALU.max))
            V.tensor_copy(row_no_i[:], row_no[:]).then_inc(rows_known, 1)
            split_weights(1, w2_hi, w2_lo)
            for c in range(2 * TPG):
                dve.wait_ge(cut_rows_in[c], 16)
                ins = V.tensor_scalar(edges_below[:, c, :],
                                      cut_row[c].rearrange("p (c t) -> p c t", t=2)[:, :, 1].bitcast(F32),
                                      bound[:, c:c + 1], None, ALU.is_lt)
            then(ins)
            then(V.tensor_reduce(edges_no[:], edges_below, AX_X, ALU.add))
            then(V.scalar_tensor_tensor(out=edges_no[:], in0=row_no[:], scalar=float(ec), in1=edges_no[:],
                                        op0=ALU.mult, op1=ALU.add))
            then(V.tensor_tensor(extra[:], edges_no[:, TPG:2 * TPG], edges_no[:, 0:TPG], ALU.subtract))
            then(V.tensor_scalar(extra[:], extra[:], float(P), 0.0, ALU.subtract, ALU.max))
            then(V.tensor_scalar(extra_i[:], extra[:], float(step_edges - 1), None, ALU.add))
            then(V.tensor_scalar(tile_info[:, :, 1], extra_i[:], step_bits, None, ALU.logical_shift_right))
            V.tensor_copy(extra[:], tile_info[:, :, 1])
            then(V.memset(steps_before[:, 0:1], 0.0))
            for i in range(TPG):
                then(V.tensor_tensor(steps_before[:, i + 1:i + 2], steps_before[:, i:i + 1], extra[:, i:i + 1],
                                     ALU.add))
            V.memset(tile_info[:, :, 3], 0).then_inc(totals_made, 1)
            dve.wait_ge(totals_spread, 1)
            V.tensor_copy(tile_info[:, :, 0], edges_no[:, 0:TPG])
            V.tensor_scalar(tile_info[:, :, 2], steps_before[:, 0:TPG], banks[0][:, 4:5], 1.0, ALU.add, ALU.add
                            ).then_inc(info_made, 1)

            def one_hot(tile):
                group, i = tile
                dve.wait_ge(edges_in_done[i], 16 * (number(group) + 1))
                wait(dve, agg_done, count(tile) - 2)
                V.tensor_scalar(onehot[i % 2][:], iota_f[:],
                                base_of[:, bass.ds(tile_no(tile), 1)],
                                edges_in[i][:, 1:2].bitcast(F32), ALU.add, ALU.is_equal).then_inc(onehot_done, 1)

            one_hot(((0, 0), 0))

            def group_dve(group):
                half = group[1] % 2
                for i in range(TPG):
                    tile = tile_of(plus(group, 1), i)
                    if exists(tile):
                        dve.wait_ge(agg_done, count(tile))
                        dve.wait_ge(x_in[1 - half][i], 16 * visits(plus(group, 1)))
                        wait(dve, ht_done, count(tile) - 2)
                        V.tensor_tensor(h_rows[i % 2][:], agg_ps[i % 2][:], x_rows[1 - half][i][:], ALU.add
                                        ).then_inc(h_done, 1)
                    tile = tile_of(plus(group, 1), i + 1)
                    if exists(tile):
                        one_hot(tile)
                    tile = tile_of(plus(group, -1), i - 1)
                    if exists(tile):
                        residual(tile)
                    tile = tile_of(plus(group, 1), i)
                    if exists(tile):
                        dve.wait_ge(ht_hi_done, count(tile))
                        V.tensor_tensor(ht_lo[1 - half][:, :, i * P:(i + 1) * P],
                                        ht_ps[i % 2][:].rearrange("p (k n) -> p k n", n=P),
                                        ht_hi[1 - half][:, :, i * P:(i + 1) * P].bitcast(F32), ALU.subtract
                                        ).then_inc(ht_lo_done, 1)
                    if group_exists(group):
                        n = width(group)
                        dve.wait_ge(r_hi_done, count((group, i)))
                        V.tensor_tensor(r_lo[half][:, i, 0:n], relu_f[i % 2][:, 0:n],
                                        r_hi[half][:, i, 0:n].bitcast(F32), ALU.subtract).then_inc(r_lo_done, 1)
                    tile = tile_of(plus(group, -1), i - 1)
                    if exists(tile):
                        scale_of(tile)

            def residual(tile):
                group, i = tile
                dve.wait_ge(l2_done, count(tile))
                dve.wait_ge(xb_done, count(tile))
                wait(dve, norm_done, count(tile) - TPG)
                V.tensor_tensor(y_rows[i], l2_ps[i % 2][:], xb_rows[group[1] % 2][i], ALU.add
                                ).then_inc(y_done, 1)
                dve.wait_ge(y_done, count(tile))
                V.bn_stats(bn_parts[i][:], y_rows[i]).then_inc(bn_done, 1)
                wait_apart(dve, (bn_done, count(tile)))
                V.bn_aggr(mean_var[i][:], bn_parts[i][:]).then_inc(stats_done, 1)

            def scale_of(tile):
                _, i = tile
                dve.wait_ge(std_done, count(tile))
                V.reciprocal(rstd[i][:], std[i][:]).then_inc(rstd_done, 1)
                dve.wait_ge(rstd_done, count(tile))
                V.tensor_scalar(neg_mean[i][:], mean_var[i][:, 0:1], rstd[i][:], -1.0, ALU.mult, ALU.mult
                                ).then_inc(neg_mean_done, 1)

            over_groups(dve, group_dve)

        @block.tensor
        def _(pe):
            pe.wait_ge(step_dve, 1)
            pe.wait_ge(drops_done, 1)
            nc.tensor.matmul(banks[0][0:1, 0:1], drops_sum[:], ones[0:er, 0:1], start=True, stop=True
                             ).then_inc(drops_counted, 1)
            for a in range(2):
                nc.tensor.matmul(banks[2 + a][:, 0:1], ones[:], ones[:, 0:1], start=True, stop=True
                                 ).then_inc(more_used[a], 1)
            pe.wait_ge(diag_made, 1)
            nc.tensor.matmul(banks[1][:, 0:er], ones[0:er, :], first_diag[:], start=True, stop=True
                             ).then_inc(firsts_spread, 1)
            pe.wait_ge(totals_made, 1)
            nc.tensor.matmul(banks[0][:, 4:5], below[:], steps_before[:, TPG:TPG + 1], start=True, stop=True
                             ).then_inc(totals_spread, 1)
            pe.wait_ge(info_made, 1)
            pe.wait_ge(w_lo_done, 2)
            pe.wait_ge(table_in, 16)

            def aggregate(tile):
                steps = steps_of(pe, tile)
                i = tile[1]
                bank = agg_ps[i % 2]
                pe.wait_ge(onehot_done, count(tile))
                pe.wait_ge(nbr_hi_done, count(tile))
                wait(pe, h_done, count(tile) - 2)
                nc.tensor.matmul(bank[:], onehot[i % 2][:], nbr_hi[i % 2][:], start=True, stop=False)
                with pe.If(steps > 0):
                    before = before_of(pe, tile)
                    with pe.Fori(0, steps) as k:
                        for a in range(2):
                            pe.wait_ge(more_nbr_in[a], 16 * (before + k + 1))
                            pe.wait_ge(more_onehot_done[a], before + k + 1)
                            nc.tensor.matmul(bank[:], more_onehot[a][:], more_nbr[a][:], start=False, stop=False
                                             ).then_inc(more_used[a], 1)
                    pe.nop()
                pe.wait_ge(nbr_lo_done, count(tile))
                nc.tensor.matmul(bank[:], onehot[i % 2][:], nbr_lo[i % 2][:], start=False, stop=True
                                 ).then_inc(agg_done, 1)

            def transpose(tile):
                i = tile[1]
                pe.wait_ge(h_done, count(tile))
                wait(pe, ht_lo_done, count(tile) - 2)
                for k in range(kb_n):
                    ins = nc.tensor.transpose(ht_ps[i % 2][:, k * P:(k + 1) * P], h_rows[i % 2][:, k * P:(k + 1) * P],
                                              ident[:])
                ins.then_inc(ht_done, 1)

            def layer1(group, f):
                half, n = group[1] % 2, width(group)
                tiles = last_tiles if is_last(group) else TPG
                pe.wait_ge(ht_lo_done, count((group, tiles - 1)))
                wait(pe, relu_done, count((group, f)) - 2)
                terms = [(w, h[half]) for w, h in ((w1_hi, ht_hi), (w1_hi, ht_lo), (w1_lo, ht_hi))]
                for t, (w, h) in enumerate(terms):
                    for k in range(kb_n):
                        ins = nc.tensor.matmul(l1_ps[f % 2][:, 0:n], w[:, k, f * P:(f + 1) * P], h[:, k, 0:n],
                                               start=(t == 0 and k == 0), stop=(t == 2 and k == kb_n - 1))
                ins.then_inc(l1_done, 1)

            def layer2(tile):
                group, i = tile
                half = group[1] % 2
                pe.wait_ge(r_lo_done, count((group, TPG - 1)))
                wait(pe, y_done, count(tile) - 2)
                terms = [(r[half], w) for r, w in ((r_hi, w2_hi), (r_lo, w2_hi), (r_hi, w2_lo))]
                for t, (r, w) in enumerate(terms):
                    for k in range(kb_n):
                        ins = nc.tensor.matmul(l2_ps[i % 2][:], r[:, k, i * P:(i + 1) * P], w[:, k, :],
                                               start=(t == 0 and k == 0), stop=(t == 2 and k == kb_n - 1))
                ins.then_inc(l2_done, 1)

            def group_products(group):
                for i in range(TPG):
                    tile = tile_of(plus(group, 1), i)
                    if exists(tile):
                        aggregate(tile)
                    if group_exists(group):
                        layer1(group, i)
                    if exists(tile):
                        transpose(tile)
                    tile = tile_of(plus(group, -1), i)
                    if exists(tile):
                        layer2(tile)

            over_groups(pe, group_products)


_INS = ["x", "src", "dst", "L0_gnn_W1", "L0_gnn_b1", "L0_gnn_W2", "L0_gnn_b2"]


def kernel(**inputs):
    import numpy as _np
    import concourse.bacc as _bacc
    from concourse import mybir as _mybir
    from concourse.bass_utils import run_bass_kernel_spmd as _run

    nc = _bacc.Bacc("TRN2", target_bir_lowering=False, num_devices=1)
    arrays, args = {}, []
    for name in _INS:
        a = _np.ascontiguousarray(inputs[name])
        arrays[f"in_{name}_dram"] = a
        args.append(nc.dram_tensor(f"in_{name}_dram", a.shape, _mybir.dt.from_np(a.dtype), kind="ExternalInput").ap())
    out = nc.dram_tensor("out_dram", inputs["x"].shape, _mybir.dt.float32, kind="ExternalOutput").ap()
    gnn_layer_with_residual_norm(nc, *args, out)
    r = _run(nc, [arrays], core_ids=[0])
    return r.results[0]["out_dram"]
```

```python
from contextlib import ExitStack

import concourse.bass as bass
from concourse import mybir

ALU = mybir.AluOpType
ACT = mybir.ActivationFunctionType
F32 = mybir.dt.float32
F32R = mybir.dt.float32r
I32 = mybir.dt.int32
U32 = mybir.dt.uint32
AX_X = mybir.AxisListType.X

P = 128
TPG = 4
EPS = 1e-5


def gnn_layer_with_residual_norm(nc, x, src, dst, w1, b1, w2, b2, out):
    n_nodes, d = x.shape
    n_edges = src.shape[0]
    kb_n = d // P
    gw = TPG * P
    last = n_nodes // gw
    last_tiles = -(-(n_nodes - last * gw) // P)
    last_base = n_nodes - last_tiles * P
    last_skip = last * gw - last_base
    n_tiles = last * TPG + last_tiles
    assert d == gw and 0 < last_tiles < TPG and 0 <= last_skip < P and last < P
    half_p = P // 2
    er = 125
    ec = n_edges // er
    assert er * ec == n_edges
    step_edges = 2 * P
    step_bits = step_edges.bit_length() - 1
    pad_edges = 4 * P
    max_steps = n_edges // step_edges + 1
    first_looped = 2
    n_pairs = (last - 3 - first_looped + 1) // 2
    after_loop = first_looped + 2 * n_pairs
    assert n_pairs >= 1

    edge_pairs = nc.dram_tensor("edge_pairs", (n_edges + step_edges * (max_steps + 2), 2), U32, kind="Internal").ap()
    tile_table = nc.dram_tensor("tile_table", (P * TPG * 4,), I32, kind="Internal").ap()

    ctx = ExitStack()
    with ctx:
        def sb(name, shape, dt):
            return ctx.enter_context(nc.sbuf_tensor(name, shape, dt))

        def sem(name):
            return ctx.enter_context(nc.semaphore(name))

        def sems(name, n):
            return [sem(f"{name}{i}") for i in range(n)]

        w_stage = sb("w_stage", [P, kb_n, d], F32)
        w1_hi, w1_lo = sb("w1_hi", [P, kb_n, d], F32R), sb("w1_lo", [P, kb_n, d], F32R)
        w2_hi, w2_lo = sb("w2_hi", [P, kb_n, d], F32R), sb("w2_lo", [P, kb_n, d], F32R)
        b1_col = sb("b1_col", [P, kb_n], F32)
        b2_rows = sb("b2_rows", [P, d], F32)
        x_rows = [[sb(f"x_rows{a}{i}", [P, d], F32) for i in range(TPG)] for a in range(2)]
        xb_mem = sb("xb_mem", [P, 2 * TPG * d], F32)
        xb_rows = [[xb_mem[:, (TPG * a + i) * d:(TPG * a + i + 1) * d] for i in range(TPG)] for a in range(2)]
        h_rows = [sb(f"h_rows{i}", [P, d], F32) for i in range(2)]
        ht_hi = [sb(f"ht_hi{a}", [P, kb_n, gw], F32R) for a in range(2)]
        ht_lo = [sb(f"ht_lo{a}", [P, kb_n, gw], F32R) for a in range(2)]
        relu_f = [sb(f"relu_f{i}", [P, gw], F32) for i in range(2)]
        r_hi = [sb(f"r_hi{a}", [P, kb_n, gw], F32R) for a in range(2)]
        r_lo = [sb(f"r_lo{a}", [P, kb_n, gw], F32R) for a in range(2)]
        edges_in = [sb(f"edges_in{i}", [P, 2], U32) for i in range(TPG)]
        nbr = [sb(f"nbr{i}", [P, d], F32) for i in range(TPG)]
        hi_lo = [sb(f"hi_lo{i}", [P, d], F32R) for i in range(2)]
        lo_hi = [sb(f"lo_hi{i}", [P, d], F32R) for i in range(2)]
        onehot = [sb(f"onehot{i}", [P, P], F32R) for i in range(2)]
        more_in = sb("more_in", [P, 2, 2], U32)
        more_rel = [sb(f"more_rel{a}", [P, 1], F32) for a in range(2)]
        more_base = [sb(f"more_base{i}", [P, 1], F32) for i in range(TPG)]
        more_nbr = [sb(f"more_nbr{a}", [P, d], F32) for a in range(2)]
        more_onehot = [sb(f"more_onehot{a}", [P, P], F32) for a in range(2)]
        y_mem, o_mem = sb("y_mem", [P, TPG * d], F32), sb("o_mem", [P, TPG * d], F32)
        y_rows = [y_mem[:, i * d:(i + 1) * d] for i in range(TPG)]
        o_rows = [o_mem[:, i * d:(i + 1) * d] for i in range(TPG)]
        bn_parts = [sb(f"bn_parts{i}", [P, 6], F32) for i in range(TPG)]
        mean_var = [sb(f"mean_var{i}", [P, 2], F32) for i in range(TPG)]
        std = [sb(f"std{i}", [P, 1], F32) for i in range(TPG)]
        rstd = [sb(f"rstd{i}", [P, 1], F32) for i in range(TPG)]
        neg_mean = [sb(f"neg_mean{i}", [P, 1], F32) for i in range(TPG)]
        eps_col = sb("eps_col", [P, 1], F32)
        base_of = sb("base_of", [P, n_tiles], F32)
        iota_i = sb("iota_i", [P, n_tiles], I32)
        iota_f = sb("iota_f", [P, P], F32)
        iota_p_i, iota_p = sb("iota_p_i", [P, 1], I32), sb("iota_p", [P, 1], F32)
        ident = sb("ident", [P, P], F32)
        below = sb("below", [P, P], F32)
        ones = sb("ones", [P, P], F32)
        n_bounds = TPG + 1
        dst_i, src_i = sb("dst_i", [er, ec], I32), sb("src_i", [er, ec], I32)
        dst_next = sb("dst_next", [er, ec], I32)
        drops = sb("drops", [er, ec], F32)
        drops_sum = sb("drops_sum", [er, 1], F32)
        unsorted_i = sb("unsorted_i", [1, 1], I32)
        pair_rows = sb("pair_rows", [er, ec, 2], U32)
        pad_rows = sb("pad_rows", [P, pad_edges // P, 2], U32)
        row_first = sb("row_first", [er, 2], U32)
        first_diag = sb("first_diag", [er, er], F32)
        bound_i, bound = sb("bound_i", [P, n_bounds], I32), sb("bound", [P, n_bounds], F32)
        last_shift = sb("last_shift", [P, 1], F32)
        rows_below = o_mem[:, 0:n_bounds * er].rearrange("p (c r) -> p c r", r=er)
        row_no, row_no_i = sb("row_no", [P, n_bounds], F32), sb("row_no_i", [P, n_bounds], U32)
        cut_row = [xb_mem[:, 2 * ec * c:2 * ec * (c + 1)].bitcast(U32) for c in range(n_bounds)]
        edges_below = y_mem[:, 0:n_bounds * ec].rearrange("p (c r) -> p c r", r=ec)
        edges_no = sb("edges_no", [P, n_bounds], F32)
        tile_edges, over_half = sb("tile_edges", [P, TPG], F32), sb("over_half", [P, TPG], F32)
        sort_w, sort_parts = 5 * ec, er // 5
        own_no, own_dst2 = sb("own_no", [er, ec], F32), sb("own_dst2", [er, ec], F32)
        place, place_part = sb("place", [er, ec], F32), sb("place_part", [er, 1], F32)
        other_i, other_dst2, is_before, goes_before = (xb_mem[0:er, n * sort_w:(n + 1) * sort_w] for n in range(4))
        other_i = other_i.bitcast(I32)
        local_no, local_no_i = y_mem[0:er, 0:sort_w], y_mem[0:er, sort_w:2 * sort_w].bitcast(I32)
        own_no_i = sb("own_no_i", [er, ec], I32)
        pair_col, place_col = sb("pair_col", [er, 2], U32), sb("place_col", [er, 1], U32)
        extra, extra_i = sb("extra", [P, TPG], F32), sb("extra_i", [P, TPG], I32)
        steps_i = sb("steps_i", [P, TPG], I32)
        steps_before = sb("steps_before", [P, TPG + 1], F32)
        tile_info = sb("tile_info", [P, TPG, 4], I32)
        tile_row = sb("tile_row", [1, P * TPG * 4], I32)

        banks = [ctx.enter_context(nc.psum_tensor(f"bank{i}", [P, d], F32)) for i in range(8)]
        agg_ps, ht_ps, l1_ps, l2_ps = banks[0:2], banks[2:4], banks[4:6], banks[6:8]

        w_in = sems("w_in", 2)
        consts_in = sem("consts_in")
        eps_set = sem("eps_set")
        w_hi_done, w_lo_done = sem("w_hi_done"), sem("w_lo_done")
        iotas_done = sem("iotas_done")
        step_dve = sem("step_dve")
        edges_loaded = sem("edges_loaded")
        next_cleared, next_loaded = sem("next_cleared"), sem("next_loaded")
        pairs_made, pairs_stored = sem("pairs_made"), sem("pairs_stored")
        drops_done, drops_counted = sem("drops_done"), sem("drops_counted")
        flag_made = sem("flag_made")
        order_final = sem("order_final")
        firsts_in, diag_made, firsts_spread = sem("firsts_in"), sem("diag_made"), sem("firsts_spread")
        rows_known, cut_rows_in = sem("rows_known"), sems("cut_rows_in", n_bounds)
        totals_made, totals_spread = sem("totals_made"), sem("totals_spread")
        info_made, info_stored, table_in = sem("info_made"), sem("info_stored"), sem("table_in")
        x_in = [sems(f"x_in{a}", TPG) for a in range(2)]
        edges_in_done = sems("edges_in_done", TPG)
        nbr_in = sems("nbr_in", TPG)
        nbr_hi_done, onehot_done = sem("nbr_hi_done"), sem("onehot_done")
        lo_last_done, lo_first_done = sem("lo_last_done"), sem("lo_first_done")
        agg_done, h_done, ht_done = sem("agg_done"), sem("h_done"), sem("ht_done")
        ht_hi_done, ht_lo_done = sem("ht_hi_done"), sem("ht_lo_done")
        l1_done, relu_done = sem("l1_done"), sem("relu_done")
        r_hi_done, r_lo_done = sem("r_hi_done"), sem("r_lo_done")
        l2_done, xb_done, y_done = sem("l2_done"), sem("xb_done"), sem("y_done")
        bn_done, stats_done, std_done = sem("bn_done"), sem("stats_done"), sem("std_done")
        rstd_done, neg_mean_done = sem("rstd_done"), sem("neg_mean_done")
        norm_done = sem("norm_done")
        stored = sems("stored", TPG)
        more_edges_in = sem("more_edges_in")
        more_rel_done = sems("more_rel_done", 2)
        more_base_done = sem("more_base_done")
        more_nbr_in = sems("more_nbr_in", 2)
        more_onehot_done = sems("more_onehot_done", 2)
        more_used = sems("more_used", 2)
        sort_step = sem("sort_step")
        sort_part_used, sort_part_in = sem("sort_part_used"), sem("sort_part_in")
        sort_column, sort_put = sem("sort_column"), sem("sort_put")

        base_of_made = 2

        block = ctx.enter_context(nc.Block())

        def plus(group, c):
            return group[0], group[1] + c

        def number(group):
            return 2 * group[0] + group[1]

        def visits(group):
            return group[0] + group[1] // 2 + 1

        def tile_of(group, i):
            return plus(group, i // TPG), i % TPG

        def looped(group):
            return not isinstance(group[0], int)

        def is_last(group):
            return not looped(group) and group[1] == last

        def exists(tile):
            group, i = tile
            return looped(group) or 0 <= group[1] < last or (group[1] == last and i < last_tiles)

        def group_exists(group):
            return looped(group) or 0 <= group[1] <= last

        def tile_no(tile):
            group, i = tile
            return 2 * TPG * group[0] + TPG * group[1] + i

        def count(tile):
            return tile_no(tile) + 1

        def width(group):
            return last_tiles * P if is_last(group) else gw

        def rows_of(tile):
            group, i = tile
            if is_last(group):
                return bass.ds(last_base + i * P, P)
            return bass.ds(gw * (last - 1 - group[1]) + i * P - 2 * gw * group[0], P)

        def wait(eng, semaphore, value):
            if isinstance(value, int) and value <= 0:
                return
            eng.wait_ge(semaphore, value)

        def wait_apart(eng, *waits):
            for _, value in waits:
                eng.compute_val(value)
            eng.wait_ge(flag_made, 1)
            for semaphore, value in waits:
                wait(eng, semaphore, value)

        def over_groups(eng, body):
            for c in range(-1, first_looped):
                body((0, c))
            with eng.Fori(0, n_pairs) as m:
                body((m, first_looped))
                body((m, first_looped + 1))
            for c in range(after_loop, last + 2):
                body((0, c))

        def first_of(eng, tile):
            return eng.value_load(tile_row[0:1, bass.ds(4 * tile_no(tile), 1)], min_val=0, max_val=n_edges)

        def kind_of(eng, tile):
            return eng.value_load(tile_row[0:1, bass.ds(4 * tile_no(tile) + 1, 1)], min_val=0, max_val=max_steps + 1)

        def before_of(eng, tile):
            return eng.value_load(tile_row[0:1, bass.ds(4 * tile_no(tile) + 2, 1)], min_val=1,
                                  max_val=max_steps + n_tiles)

        def second_half_of(eng, tile):
            return eng.value_load(tile_row[0:1, bass.ds(4 * tile_no(tile) + 3, 1)], min_val=0,
                                  max_val=n_edges + half_p)

        @block.sync
        def _(sp):
            sp.dma_start(dst_i[:], dst.rearrange("(r c) -> r c", c=ec)).then_inc(edges_loaded, 16)
            sp.dma_start(src_i[:], src.rearrange("(r c) -> r c", c=ec)).then_inc(edges_loaded, 16)
            sp.wait_ge(next_cleared, 1)
            sp.dma_start(dst_next[0:er - 1, :], dst[1:1 + (er - 1) * ec].rearrange("(r c) -> r c", c=ec)
                         ).then_inc(next_loaded, 16)
            sp.dma_start(dst_next[er - 1:er, 0:ec - 1], dst[(er - 1) * ec + 1:n_edges].rearrange("(r c) -> r c", r=1)
                         ).then_inc(next_loaded, 16)
            sp.wait_ge(pairs_made, 1)
            sp.dma_start(edge_pairs[0:n_edges, :].rearrange("(r c) t -> r c t", c=ec), pair_rows[:]
                         ).then_inc(pairs_stored, 16)
            sp.dma_start(edge_pairs[n_edges:n_edges + pad_edges, :].rearrange("(r c) t -> r c t", r=P), pad_rows[:]
                         ).then_inc(pairs_stored, 16)
            sp.wait_ge(order_final, 1)
            sp.dma_start(row_first[:], edge_pairs[0:n_edges, :].rearrange("(r c) t -> r c t", c=ec)[:, 0, :]
                         ).then_inc(firsts_in, 16)
            for i in range(TPG):
                sp.dma_start(x_rows[0][i][:], x[rows_of(((0, 0), i)), :]).then_inc(x_in[0][i], 16)
            sp.wait_ge(info_made, 1)
            sp.dma_start(tile_table.rearrange("(p c) -> p c", p=P), tile_info[:].rearrange("p t c -> p (t c)")
                         ).then_inc(info_stored, 16)
            sp.wait_ge(info_stored, 16)
            sp.dma_start(tile_row[:], tile_table.rearrange("(o c) -> o c", o=1)).then_inc(table_in, 16)
            sp.wait_ge(table_in, 16)

            def load_edges(tile):
                i = tile[1]
                first, second = first_of(sp, tile), second_half_of(sp, tile)
                wait_apart(sp, (onehot_done, count(tile) - TPG), (nbr_in[i], 16 * number(tile[0])))
                sp.dma_start(edges_in[i][0:half_p, :], edge_pairs[bass.ds(first, half_p), :]
                             ).then_inc(edges_in_done[i], 16)
                sp.dma_start(edges_in[i][half_p:P, :], edge_pairs[bass.ds(second, half_p), :]
                             ).then_inc(edges_in_done[i], 16)

            def load_further_edges(tile):
                kind = kind_of(sp, tile)
                with sp.If(kind > 1):
                    first, before = first_of(sp, tile), before_of(sp, tile)
                    with sp.Fori(0, kind - 1) as k:
                        wait_apart(sp, *[(more_rel_done[a], before + k) for a in range(2)],
                                   *[(more_nbr_in[a], 16 * (before + k)) for a in range(2)])
                        sp.dma_start(more_in[:], edge_pairs[bass.ds(first + step_edges * k + P, step_edges), :]
                                     .rearrange("(a p) t -> p a t", p=P)).then_inc(more_edges_in, 16)
                    sp.nop()

            for i in range(TPG):
                load_edges(((0, 0), i))
            for i in range(2):
                load_further_edges(((0, 0), i))

            def group_loads(group):
                for i in range(TPG):
                    ahead = tile_of(plus(group, 2), i)
                    if exists(ahead):
                        load_edges(ahead)
                    tile = tile_of(plus(group, 1), i + 2)
                    if exists(tile):
                        load_further_edges(tile)
                    if exists(ahead):
                        a = ahead[0][1] % 2
                        wait_apart(sp, (xb_done, count(tile_of(group, i))))
                        sp.dma_start(x_rows[a][i][:], x[rows_of(ahead), :]).then_inc(x_in[a][i], 16)

            over_groups(sp, group_loads)

        @block.gpsimd
        def _(pool):
            nc.gpsimd.iota(iota_i[:, 0:last * TPG], pattern=[[-gw, last], [P, TPG]], base=(last - 1) * gw,
                           channel_multiplier=0).then_inc(iotas_done, 1)
            nc.gpsimd.iota(iota_i[:, last * TPG:], pattern=[[P, last_tiles]], base=last_base,
                           channel_multiplier=0).then_inc(iotas_done, 1)
            nc.gpsimd.iota(iota_p_i[:], pattern=[[0, 1]], base=0, channel_multiplier=1).then_inc(iotas_done, 1)
            nc.gpsimd.iota(bound_i[:], pattern=[[P, n_bounds]], base=(last - 1) * gw, channel_multiplier=-gw
                           ).then_inc(iotas_done, 1)
            nc.gpsimd.iota(iota_f[:], pattern=[[1, P]], base=0, channel_multiplier=0,
                           allow_small_or_imprecise_dtypes=True).then_inc(iotas_done, 1)

            def put_sorted():
                with pool.Fori(0, sort_parts) as q:
                    wait_apart(pool, (sort_part_used, q + 1))
                    pool.dma_start(other_i, dst[bass.ds(q * sort_w, sort_w)].rearrange("(o c) -> o c", o=1)
                                   .to_broadcast([er, sort_w])).then_inc(sort_part_in, 16)
                pool.wait_ge(sort_part_used, sort_parts + 1)
                with pool.Fori(0, ec) as j:
                    nc.gpsimd.tensor_copy(pair_col[:], pair_rows[:, bass.ds(j, 1), :].rearrange("p o t -> p (o t)"))
                    nc.gpsimd.tensor_copy(place_col[:], place[:, bass.ds(j, 1)]).then_inc(sort_column, 1)
                    wait_apart(pool, (sort_column, j + 1))
                    pool.indirect_dma_start(edge_pairs, bass.IndirectOffsetOnAxis(ap=place_col[:], axis=0),
                                            pair_col[:], None).then_inc(sort_put, 16)
                    pool.wait_ge(sort_put, 16 * (j + 1))

            nc.gpsimd.iota(own_no_i[:], pattern=[[1, ec]], base=0, channel_multiplier=ec).then_inc(iotas_done, 1)
            nc.gpsimd.iota(local_no_i, pattern=[[1, sort_w]], base=0, channel_multiplier=0).then_inc(iotas_done, 1)
            for a in range(2):
                pool.dma_start(more_nbr[a][:, 0:16], x[0:P, 0:16]).then_inc(more_nbr_in[a], 16)
                nc.gpsimd.memset(more_onehot[a][:], 0.0).then_inc(more_onehot_done[a], 1)
                nc.gpsimd.memset(more_rel[a][:], 0.0).then_inc(more_rel_done[a], 1)
            pool.wait_ge(flag_made, 1)
            pool.wait_ge(pairs_stored, 32)
            unsorted = pool.value_load(unsorted_i[:], min_val=0, max_val=n_edges)
            with pool.If(unsorted > 0):
                put_sorted()
                pool.nop()
            nc.gpsimd.memset(more_base[0][:], 0.0).then_inc(order_final, 1)
            pool.wait_ge(rows_known, 1)
            edge_rows = edge_pairs[0:n_edges, :].rearrange("(r c) t -> r (c t)", c=ec)
            for c in range(n_bounds):
                pool.indirect_dma_start(cut_row[c], None, edge_rows,
                                        bass.IndirectOffsetOnAxis(ap=row_no_i[:, c:c + 1], axis=0)
                                        ).then_inc(cut_rows_in[c], 16)

            def gather(tile):
                i = tile[1]
                wait_apart(pool, (edges_in_done[i], 32 * (number(tile[0]) + 1)), (nbr_hi_done, count(tile) - TPG),
                           (lo_last_done, count(tile) - TPG), (lo_first_done, count(tile) - TPG))
                pool.indirect_dma_start(nbr[i][:], None, x,
                                        bass.IndirectOffsetOnAxis(ap=edges_in[i][:, 0:1], axis=0)
                                        ).then_inc(nbr_in[i], 16)

            def split_lo_first(tile):
                i = tile[1]
                pool.wait_ge(nbr_hi_done, count(tile))
                wait(pool, agg_done, count(tile) - 2)
                nc.gpsimd.tensor_tensor(lo_hi[i % 2][0:half_p, :], nbr[i][0:half_p, :],
                                        hi_lo[i % 2][0:half_p, :].bitcast(F32), ALU.subtract
                                        ).then_inc(lo_first_done, 1)

            def further_steps(tile):
                kind = kind_of(pool, tile)
                base = more_base[tile[1]]
                nc.gpsimd.tensor_copy(base[:], base_of[:, bass.ds(tile_no(tile), 1)]).then_inc(more_base_done, 1)
                with pool.If(kind > 1):
                    before = before_of(pool, tile)
                    wait_apart(pool, (more_base_done, count(tile)))
                    with pool.Fori(0, kind - 1) as k:
                        for a in range(2):
                            wait_apart(pool, (more_edges_in, 16 * (before + k)), (more_used[a], before + k))
                            pool.indirect_dma_start(more_nbr[a][:], None, x,
                                                    bass.IndirectOffsetOnAxis(ap=more_in[:, a, 0:1], axis=0)
                                                    ).then_inc(more_nbr_in[a], 16)
                        for a in range(2):
                            nc.gpsimd.tensor_tensor(more_rel[a][:], more_in[:, a, 1:2].bitcast(F32), base[:],
                                                    ALU.subtract).then_inc(more_rel_done[a], 1)
                        wait_apart(pool, *[(more_rel_done[a], before + k + 1) for a in range(2)])
                        for a in range(2):
                            nc.gpsimd.tensor_scalar(more_onehot[a][:], iota_f[:], more_rel[a][:], None, ALU.is_equal
                                                    ).then_inc(more_onehot_done[a], 1)
                    pool.nop()

            pool.wait_ge(table_in, 16)
            pool.wait_ge(step_dve, base_of_made)
            for i in range(TPG - 1):
                gather(((0, 0), i))
            split_lo_first(((0, 0), 0))
            for i in range(2):
                further_steps(((0, 0), i))
            pool.wait_ge(consts_in, 32)

            def group_edges(group):
                for i in range(TPG):
                    for tile, work in ((tile_of(plus(group, 1), i + 3), gather),
                                       (tile_of(plus(group, 1), i + 1), split_lo_first),
                                       (tile_of(plus(group, 1), i + 2), further_steps)):
                        if exists(tile):
                            work(tile)
                    tile = tile_of(group, i)
                    if exists(tile):
                        a = group[1] % 2
                        pool.wait_ge(x_in[a][i], 16 * visits(group))
                        pool.wait_ge(h_done, count(tile))
                        wait(pool, y_done, count(tile) - 2 * TPG)
                        nc.gpsimd.tensor_tensor(xb_rows[a][i], x_rows[a][i][:], b2_rows[:], ALU.add
                                                ).then_inc(xb_done, 1)

            over_groups(pool, group_edges)

        @block.scalar
        def _(act):
            act.wait_ge(next_loaded, 32)
            act.dma_start(w_stage[:], w1.rearrange("(k p) n -> p k n", p=P)).then_inc(w_in[0], 16)
            act.dma_start(b1_col[:], b1.rearrange("(k p) -> p k", p=P),
                          allow_slow_non_contiguous=True).then_inc(consts_in, 16)
            act.dma_start(b2_rows[:], b2.rearrange("(o n) -> o n", o=1).to_broadcast([P, d])
                          ).then_inc(consts_in, 16)
            for n, (hi, w) in enumerate(((w1_hi, w2), (w2_hi, None))):
                act.wait_ge(w_in[n], 16)
                nc.scalar.copy(hi[:], w_stage[:]).then_inc(w_hi_done, 1)
                if w is not None:
                    act.wait_ge(w_lo_done, 1)
                    act.dma_start(w_stage[:], w.rearrange("(k p) n -> p k n", p=P)).then_inc(w_in[1], 16)
            act.wait_ge(consts_in, 32)
            act.wait_ge(eps_set, 1)

            def split_hi(tile):
                i = tile[1]
                act.wait_ge(nbr_in[i], 16 * (number(tile[0]) + 1))
                wait(act, agg_done, count(tile) - 2)
                nc.scalar.copy(hi_lo[i % 2][0:half_p, :], nbr[i][0:half_p, :])
                nc.scalar.copy(lo_hi[i % 2][half_p:P, :], nbr[i][half_p:P, :]).then_inc(nbr_hi_done, 1)

            split_hi(((0, 0), 0))

            def group_act(group):
                for i in range(TPG):
                    half = group[1] % 2
                    n = width(group) if group_exists(group) else 0
                    block_no = count((group, i))
                    tile = tile_of(plus(group, 1), i + 1)
                    if exists(tile):
                        split_hi(tile)
                    if group_exists(group):
                        act.wait_ge(l1_done, block_no)
                        wait(act, r_lo_done, block_no - 2)
                        nc.scalar.activation(relu_f[i % 2][:, 0:n], l1_ps[i % 2][:, 0:n], ACT.Relu,
                                             bias=b1_col[:, i:i + 1]).then_inc(relu_done, 1)
                    tile = tile_of(plus(group, 1), i)
                    if exists(tile):
                        act.wait_ge(ht_done, count(tile))
                        nc.scalar.copy(ht_hi[1 - half][:, :, i * P:(i + 1) * P],
                                       ht_ps[i % 2][:].rearrange("p (k n) -> p k n", n=P)).then_inc(ht_hi_done, 1)
                    if group_exists(group):
                        act.wait_ge(relu_done, block_no)
                        wait(act, l2_done, count((plus(group, -2), TPG - 1)))
                        nc.scalar.copy(r_hi[half][:, i, 0:n], relu_f[i % 2][:, 0:n]).then_inc(r_hi_done, 1)
                    tile = tile_of(plus(group, -1), i - 2)
                    if exists(tile):
                        normalise(tile)
                    tile = tile_of(plus(group, -1), i - 1)
                    if exists(tile):
                        act.wait_ge(stats_done, count(tile))
                        nc.scalar.activation(std[tile[1]][:], mean_var[tile[1]][:, 1:2], ACT.Sqrt,
                                             bias=eps_col[:]).then_inc(std_done, 1)

            def normalise(tile):
                group, i = tile
                act.wait_ge(neg_mean_done, count(tile))
                wait(act, stored[i], 16 * number(group))
                nc.scalar.activation(o_rows[i], y_rows[i], ACT.Identity, bias=neg_mean[i][:],
                                     scale=rstd[i][:]).then_inc(norm_done, 1)
                act.wait_ge(norm_done, count(tile))
                if is_last(group) and i == 0:
                    if last_skip < P:
                        act.dma_start(out[last * gw:last_base + P, :], o_rows[i][last_skip:P, :]
                                      ).then_inc(stored[i], 16)
                else:
                    act.dma_start(out[rows_of(tile), :], o_rows[i]).then_inc(stored[i], 16)

            over_groups(act, group_act)
            for tile in (tile_of((0, last + 1), i - 2) for i in range(TPG)):
                if exists(tile):
                    normalise(tile)
            for i in range(TPG):
                act.wait_ge(stored[i], 16 * (last + (1 if i < last_tiles else 0)))

        @block.vector
        def _(dve):
            chain = [0]

            def then(instruction):
                chain[0] += 1
                instruction.then_inc(step_dve, 1)
                dve.wait_ge(step_dve, chain[0])

            V = nc.vector
            V.memset(dst_next[:], 1 << 24).then_inc(next_cleared, 1)
            V.memset(eps_col[:], EPS).then_inc(eps_set, 1)
            V.memset(pad_rows[:, :, 0], 0)
            V.memset(pad_rows[:, :, 1].bitcast(F32), -1.0)
            then(V.memset(ones[:], 1.0))
            dve.wait_ge(iotas_done, 5)
            V.tensor_copy(bound[:], bound_i[:])
            V.tensor_copy(base_of[:], iota_i[:])
            then(V.tensor_copy(iota_p[:], iota_p_i[:]))
            V.tensor_scalar(ident[:], iota_f[:], iota_p[:], None, ALU.is_equal)
            V.tensor_scalar(below[:], iota_f[:], iota_p[:], None, ALU.is_gt)
            then(V.tensor_scalar(last_shift[:], iota_p[:], float(last), float(last_base + gw), ALU.is_equal, ALU.mult))
            then(V.tensor_scalar(bound[:], bound[:], last_shift[:], None, ALU.add))

            dve.wait_ge(edges_loaded, 32)
            V.tensor_copy(pair_rows[:, :, 0], src_i[:])
            V.tensor_copy(pair_rows[:, :, 1].bitcast(F32), dst_i[:]).then_inc(pairs_made, 1)
            dve.wait_ge(next_loaded, 32)
            then(V.tensor_tensor(drops[:], dst_next[:], dst_i[:], ALU.is_lt))
            V.tensor_reduce(drops_sum[:], drops[:], AX_X, ALU.add).then_inc(drops_done, 1)
            dve.wait_ge(drops_counted, 1)
            V.tensor_copy(unsorted_i[:], banks[0][0:1, 0:1]).then_inc(flag_made, 1)

            def split_weights(n, hi, lo):
                dve.wait_ge(w_hi_done, n + 1)
                V.tensor_tensor(lo[:], w_stage[:], hi[:].bitcast(F32), ALU.subtract).then_inc(w_lo_done, 1)

            split_weights(0, w1_hi, w1_lo)
            def find_places():
                per_column, per_part = 4, 2

                def step(instruction, value):
                    instruction.then_inc(sort_step, 1)
                    dve.wait_ge(sort_step, value)

                V.tensor_copy(own_no[:], own_no_i[:])
                V.tensor_copy(local_no, local_no_i)
                V.memset(place[:], 0.0)
                step(V.tensor_scalar(own_dst2[:], dst_i[:], 2.0, None, ALU.mult), 1)
                V.memset(place_part[:], 0.0).then_inc(sort_part_used, 1)
                with dve.Fori(0, sort_parts) as q:
                    at_part = 1 + q * (per_part + per_column * ec)
                    dve.wait_ge(sort_part_in, 16 * (q + 1))
                    V.tensor_scalar(other_dst2, other_i, 2.0, None, ALU.mult).then_inc(sort_step, 1)
                    wait_apart(dve, (sort_step, at_part + 1))
                    with dve.Fori(0, ec) as j:
                        at = at_part + 1 + per_column * j
                        step(V.tensor_scalar(is_before, local_no, own_no[:, bass.ds(j, 1)], None, ALU.is_lt),
                             at + 1)
                        step(V.scalar_tensor_tensor(out=goes_before, in0=other_dst2,
                                                    scalar=own_dst2[:, bass.ds(j, 1)], in1=is_before,
                                                    op0=ALU.subtract, op1=ALU.is_lt), at + 2)
                        step(V.tensor_reduce(place_part[:], goes_before, AX_X, ALU.add), at + 3)
                        step(V.tensor_tensor(place[:, bass.ds(j, 1)], place[:, bass.ds(j, 1)], place_part[:],
                                             ALU.add), at + 4)
                    step(V.tensor_scalar(own_no[:], own_no[:], float(sort_w), None, ALU.subtract),
                         at_part + 2 + per_column * ec)
                    V.memset(place_part[:], 0.0).then_inc(sort_part_used, 1)

            dve.wait_ge(flag_made, 1)
            unsorted = dve.value_load(unsorted_i[:], min_val=0, max_val=n_edges)
            with dve.If(unsorted > 0):
                dve.wait_ge(iotas_done, 7)
                find_places()
                dve.nop()

            dve.wait_ge(firsts_in, 16)
            V.tensor_scalar(first_diag[:], ident[0:er, 0:er], row_first[:, 1:2].bitcast(F32), None, ALU.mult
                            ).then_inc(diag_made, 1)
            dve.wait_ge(firsts_spread, 1)
            for c in range(n_bounds):
                ins = V.tensor_scalar(rows_below[:, c, :], banks[1][:, 0:er], bound[:, c:c + 1], None, ALU.is_lt)
            then(ins)
            then(V.tensor_reduce(row_no[:], rows_below, AX_X, ALU.add))
            then(V.tensor_scalar(row_no[:], row_no[:], 1.0, 0.0, ALU.subtract, ALU.max))
            V.tensor_copy(row_no_i[:], row_no[:]).then_inc(rows_known, 1)
            split_weights(1, w2_hi, w2_lo)
            for c in range(n_bounds):
                dve.wait_ge(cut_rows_in[c], 16)
                ins = V.tensor_scalar(edges_below[:, c, :],
                                      cut_row[c].rearrange("p (c t) -> p c t", t=2)[:, :, 1].bitcast(F32),
                                      bound[:, c:c + 1], None, ALU.is_lt)
            then(ins)
            then(V.tensor_reduce(edges_no[:], edges_below, AX_X, ALU.add))
            then(V.scalar_tensor_tensor(out=edges_no[:], in0=row_no[:], scalar=float(ec), in1=edges_no[:],
                                        op0=ALU.mult, op1=ALU.add))
            then(V.tensor_tensor(tile_edges[:], edges_no[:, 1:n_bounds], edges_no[:, 0:TPG], ALU.subtract))
            V.tensor_scalar(over_half[:], tile_edges[:], float(half_p), None, ALU.is_gt)
            then(V.tensor_scalar(extra[:], tile_edges[:], float(P), 0.0, ALU.subtract, ALU.max))
            then(V.tensor_scalar(extra_i[:], extra[:], float(step_edges - 1), None, ALU.add))
            then(V.tensor_scalar(steps_i[:], extra_i[:], step_bits, None, ALU.logical_shift_right))
            V.tensor_copy(extra[:], steps_i[:])
            then(V.memset(steps_before[:, 0:1], 0.0))
            for i in range(TPG):
                then(V.tensor_tensor(steps_before[:, i + 1:i + 2], steps_before[:, i:i + 1], extra[:, i:i + 1],
                                     ALU.add))
            V.tensor_tensor(tile_info[:, :, 1], extra[:], over_half[:], ALU.add).then_inc(totals_made, 1)
            V.scalar_tensor_tensor(out=tile_info[:, :, 3], in0=over_half[:], scalar=float(half_p),
                                   in1=edges_no[:, 0:TPG], op0=ALU.mult, op1=ALU.add)
            dve.wait_ge(totals_spread, 1)
            V.tensor_copy(tile_info[:, :, 0], edges_no[:, 0:TPG])
            V.tensor_scalar(tile_info[:, :, 2], steps_before[:, 0:TPG], banks[0][:, 4:5], 1.0, ALU.add, ALU.add
                            ).then_inc(info_made, 1)

            def one_hot(tile):
                group, i = tile
                dve.wait_ge(edges_in_done[i], 32 * (number(group) + 1))
                wait(dve, agg_done, count(tile) - 2)
                V.tensor_scalar(onehot[i % 2][:], iota_f[:],
                                base_of[:, bass.ds(tile_no(tile), 1)],
                                edges_in[i][:, 1:2].bitcast(F32), ALU.add, ALU.is_equal).then_inc(onehot_done, 1)

            def split_lo_last(tile):
                i = tile[1]
                dve.wait_ge(nbr_hi_done, count(tile))
                V.tensor_tensor(hi_lo[i % 2][half_p:P, :], nbr[i][half_p:P, :],
                                lo_hi[i % 2][half_p:P, :].bitcast(F32), ALU.subtract).then_inc(lo_last_done, 1)

            one_hot(((0, 0), 0))
            split_lo_last(((0, 0), 0))

            def group_dve(group):
                half = group[1] % 2
                for i in range(TPG):
                    tile = tile_of(plus(group, 1), i)
                    if exists(tile):
                        dve.wait_ge(agg_done, count(tile))
                        dve.wait_ge(x_in[1 - half][i], 16 * visits(plus(group, 1)))
                        wait(dve, ht_done, count(tile) - 2)
                        V.tensor_tensor(h_rows[i % 2][:], agg_ps[i % 2][:], x_rows[1 - half][i][:], ALU.add
                                        ).then_inc(h_done, 1)
                    tile = tile_of(plus(group, 1), i + 1)
                    if exists(tile):
                        one_hot(tile)
                        split_lo_last(tile)
                    tile = tile_of(plus(group, -1), i - 1)
                    if exists(tile):
                        residual(tile)
                    tile = tile_of(plus(group, 1), i)
                    if exists(tile):
                        dve.wait_ge(ht_hi_done, count(tile))
                        V.tensor_tensor(ht_lo[1 - half][:, :, i * P:(i + 1) * P],
                                        ht_ps[i % 2][:].rearrange("p (k n) -> p k n", n=P),
                                        ht_hi[1 - half][:, :, i * P:(i + 1) * P].bitcast(F32), ALU.subtract
                                        ).then_inc(ht_lo_done, 1)
                    if group_exists(group):
                        n = width(group)
                        dve.wait_ge(r_hi_done, count((group, i)))
                        V.tensor_tensor(r_lo[half][:, i, 0:n], relu_f[i % 2][:, 0:n],
                                        r_hi[half][:, i, 0:n].bitcast(F32), ALU.subtract).then_inc(r_lo_done, 1)
                    tile = tile_of(plus(group, -1), i - 1)
                    if exists(tile):
                        scale_of(tile)

            def residual(tile):
                group, i = tile
                dve.wait_ge(l2_done, count(tile))
                dve.wait_ge(xb_done, count(tile))
                wait(dve, norm_done, count(tile) - TPG)
                V.tensor_tensor(y_rows[i], l2_ps[i % 2][:], xb_rows[group[1] % 2][i], ALU.add
                                ).then_inc(y_done, 1)
                dve.wait_ge(y_done, count(tile))
                V.bn_stats(bn_parts[i][:], y_rows[i]).then_inc(bn_done, 1)
                wait_apart(dve, (bn_done, count(tile)))
                V.bn_aggr(mean_var[i][:], bn_parts[i][:]).then_inc(stats_done, 1)

            def scale_of(tile):
                _, i = tile
                dve.wait_ge(std_done, count(tile))
                V.reciprocal(rstd[i][:], std[i][:]).then_inc(rstd_done, 1)
                dve.wait_ge(rstd_done, count(tile))
                V.tensor_scalar(neg_mean[i][:], mean_var[i][:, 0:1], rstd[i][:], -1.0, ALU.mult, ALU.mult
                                ).then_inc(neg_mean_done, 1)

            over_groups(dve, group_dve)

        @block.tensor
        def _(pe):
            pe.wait_ge(step_dve, 1)
            pe.wait_ge(drops_done, 1)
            nc.tensor.matmul(banks[0][0:1, 0:1], drops_sum[:], ones[0:er, 0:1], start=True, stop=True
                             ).then_inc(drops_counted, 1)
            for a in range(2):
                nc.tensor.matmul(banks[2 + a][:, 0:1], ones[:], ones[:, 0:1], start=True, stop=True
                                 ).then_inc(more_used[a], 1)
            pe.wait_ge(diag_made, 1)
            nc.tensor.matmul(banks[1][:, 0:er], ones[0:er, :], first_diag[:], start=True, stop=True
                             ).then_inc(firsts_spread, 1)
            pe.wait_ge(totals_made, 1)
            nc.tensor.matmul(banks[0][:, 4:5], below[:], steps_before[:, TPG:TPG + 1], start=True, stop=True
                             ).then_inc(totals_spread, 1)
            pe.wait_ge(info_made, 1)
            pe.wait_ge(w_lo_done, 2)
            pe.wait_ge(table_in, 16)

            def aggregate(tile):
                kind = kind_of(pe, tile)
                i = tile[1]
                bank = agg_ps[i % 2]
                nodes, first, second = onehot[i % 2], hi_lo[i % 2], lo_hi[i % 2]
                pe.wait_ge(onehot_done, count(tile))
                pe.wait_ge(lo_last_done, count(tile))
                wait(pe, h_done, count(tile) - 2)
                with pe.If(kind > 0):
                    nc.tensor.matmul(bank[:], nodes[:], first[:], start=True, stop=False)
                    with pe.If(kind > 1):
                        before = before_of(pe, tile)
                        with pe.Fori(0, kind - 1) as k:
                            for a in range(2):
                                pe.wait_ge(more_nbr_in[a], 16 * (before + k + 1))
                                pe.wait_ge(more_onehot_done[a], before + k + 1)
                                nc.tensor.matmul(bank[:], more_onehot[a][:], more_nbr[a][:], start=False, stop=False
                                                 ).then_inc(more_used[a], 1)
                        pe.nop()
                    pe.wait_ge(lo_first_done, count(tile))
                    nc.tensor.matmul(bank[:], nodes[:], second[:], start=False, stop=True).then_inc(agg_done, 1)
                with pe.Else():
                    pe.wait_ge(lo_first_done, count(tile))
                    nc.tensor.matmul(bank[:], nodes[:], first[:], start=True, stop=True).then_inc(agg_done, 1)

            def transpose(tile):
                i = tile[1]
                pe.wait_ge(h_done, count(tile))
                wait(pe, ht_lo_done, count(tile) - 2)
                for k in range(kb_n):
                    ins = nc.tensor.transpose(ht_ps[i % 2][:, k * P:(k + 1) * P], h_rows[i % 2][:, k * P:(k + 1) * P],
                                              ident[:])
                ins.then_inc(ht_done, 1)

            def layer1(group, f):
                half, n = group[1] % 2, width(group)
                tiles = last_tiles if is_last(group) else TPG
                pe.wait_ge(ht_lo_done, count((group, tiles - 1)))
                wait(pe, relu_done, count((group, f)) - 2)
                terms = [(w1_hi, ht_hi[half]), (w1_hi, ht_lo[half]), (w1_lo, ht_hi[half])]
                for k in range(kb_n):
                    for t, (w, h) in enumerate(terms):
                        ins = nc.tensor.matmul(l1_ps[f % 2][:, 0:n], w[:, k, f * P:(f + 1) * P], h[:, k, 0:n],
                                               start=(t == 0 and k == 0), stop=(t == 2 and k == kb_n - 1))
                ins.then_inc(l1_done, 1)

            def layer2(tile):
                group, i = tile
                half = group[1] % 2
                pe.wait_ge(r_lo_done, count((group, TPG - 1)))
                wait(pe, y_done, count(tile) - 2)
                terms = [(r_hi[half], w2_hi), (r_hi[half], w2_lo), (r_lo[half], w2_hi)]
                for k in range(kb_n):
                    for t, (r, w) in enumerate(terms):
                        ins = nc.tensor.matmul(l2_ps[i % 2][:], r[:, k, i * P:(i + 1) * P], w[:, k, :],
                                               start=(t == 0 and k == 0), stop=(t == 2 and k == kb_n - 1))
                ins.then_inc(l2_done, 1)

            def group_products(group):
                for i in range(TPG):
                    tile = tile_of(plus(group, 1), i)
                    if exists(tile):
                        aggregate(tile)
                    if group_exists(group):
                        layer1(group, i)
                    if exists(tile):
                        transpose(tile)
                    tile = tile_of(plus(group, -1), i)
                    if exists(tile):
                        layer2(tile)

            over_groups(pe, group_products)


_INS = ["x", "src", "dst", "L0_gnn_W1", "L0_gnn_b1", "L0_gnn_W2", "L0_gnn_b2"]


def kernel(**inputs):
    import numpy as _np
    import concourse.bacc as _bacc
    from concourse import mybir as _mybir
    from concourse.bass_utils import run_bass_kernel_spmd as _run

    nc = _bacc.Bacc("TRN2", target_bir_lowering=False, num_devices=1)
    arrays, args = {}, []
    for name in _INS:
        a = _np.ascontiguousarray(inputs[name])
        arrays[f"in_{name}_dram"] = a
        args.append(nc.dram_tensor(f"in_{name}_dram", a.shape, _mybir.dt.from_np(a.dtype), kind="ExternalInput").ap())
    out = nc.dram_tensor("out_dram", inputs["x"].shape, _mybir.dt.float32, kind="ExternalOutput").ap()
    gnn_layer_with_residual_norm(nc, *args, out)
    r = _run(nc, [arrays], core_ids=[0])
    return r.results[0]["out_dram"]
```

```python
from contextlib import ExitStack

import concourse.bass as bass
from concourse import mybir

ALU = mybir.AluOpType
ACT = mybir.ActivationFunctionType
F32 = mybir.dt.float32
F32R = mybir.dt.float32r
I32 = mybir.dt.int32
U32 = mybir.dt.uint32
AX_X = mybir.AxisListType.X

P = 128
TPG = 4
EPS = 1e-5


def gnn_layer_with_residual_norm(nc, x, src, dst, w1, b1, w2, b2, out):
    n_nodes, d = x.shape
    n_edges = src.shape[0]
    kb_n = d // P
    gw = TPG * P
    last = n_nodes // gw
    last_tiles = -(-(n_nodes - last * gw) // P)
    last_base = n_nodes - last_tiles * P
    last_skip = last * gw - last_base
    n_tiles = last * TPG + last_tiles
    assert d == gw and 0 < last_tiles < TPG and 0 <= last_skip < P and last < P
    half_p = P // 2
    er = 125
    ec = n_edges // er
    assert er * ec == n_edges
    step_edges = 2 * P
    step_bits = step_edges.bit_length() - 1
    pad_edges = 4 * P
    max_steps = n_edges // step_edges + 1
    first_looped = 2
    n_pairs = (last - 3 - first_looped + 1) // 2
    after_loop = first_looped + 2 * n_pairs
    assert n_pairs >= 1

    edge_pairs = nc.dram_tensor("edge_pairs", (n_edges + step_edges * (max_steps + 2), 2), U32, kind="Internal").ap()
    fields = 5

    ctx = ExitStack()
    with ctx:
        def sb(name, shape, dt):
            return ctx.enter_context(nc.sbuf_tensor(name, shape, dt))

        def sem(name):
            return ctx.enter_context(nc.semaphore(name))

        def sems(name, n):
            return [sem(f"{name}{i}") for i in range(n)]

        w_stage = sb("w_stage", [P, kb_n, d], F32)
        w1_hi, w1_lo = sb("w1_hi", [P, kb_n, d], F32R), sb("w1_lo", [P, kb_n, d], F32R)
        w2_hi, w2_lo = sb("w2_hi", [P, kb_n, d], F32R), sb("w2_lo", [P, kb_n, d], F32R)
        b1_col = sb("b1_col", [P, kb_n], F32)
        b2_rows = sb("b2_rows", [P, d], F32)
        x_rows = [[sb(f"x_rows{a}{i}", [P, d], F32) for i in range(TPG)] for a in range(2)]
        xb_mem = sb("xb_mem", [P, 2 * TPG * d], F32)
        xb_rows = [[xb_mem[:, (TPG * a + i) * d:(TPG * a + i + 1) * d] for i in range(TPG)] for a in range(2)]
        h_rows = [sb(f"h_rows{i}", [P, d], F32) for i in range(2)]
        ht_hi = [sb(f"ht_hi{a}", [P, kb_n, gw], F32R) for a in range(2)]
        ht_lo = [sb(f"ht_lo{a}", [P, kb_n, gw], F32R) for a in range(2)]
        relu_f = [sb(f"relu_f{i}", [P, gw], F32) for i in range(2)]
        r_hi = [sb(f"r_hi{a}", [P, kb_n, gw], F32R) for a in range(2)]
        r_lo = [sb(f"r_lo{a}", [P, kb_n, gw], F32R) for a in range(2)]
        edges_in = [sb(f"edges_in{i}", [P, 2], U32) for i in range(TPG)]
        nbr = [sb(f"nbr{i}", [P, d], F32) for i in range(TPG)]
        hi_lo = [sb(f"hi_lo{i}", [P, d], F32R) for i in range(2)]
        lo_hi = [sb(f"lo_hi{i}", [P, d], F32R) for i in range(2)]
        onehot = [sb(f"onehot{i}", [P, P], F32R) for i in range(2)]
        more_in = [sb(f"more_in{s}", [P, 2, 2], U32) for s in range(2)]
        more_src = [[sb(f"more_src{s}{a}", [P, 1], U32) for a in range(2)] for s in range(2)]
        more_rel = [[sb(f"more_rel{s}{a}", [P, 1], F32) for a in range(2)] for s in range(2)]
        more_base = [sb(f"more_base{i}", [P, 1], F32) for i in range(TPG)]
        assert kb_n == 4
        more_nbr = [[w_stage[:, 2 * s + a, :] for a in range(2)] for s in range(2)]
        more_start = sb("more_start", [P, 4, 4], F32)
        more_onehot = [[sb(f"more_onehot{s}{a}", [P, P], F32) for a in range(2)] for s in range(2)]
        y_mem, o_mem = sb("y_mem", [P, TPG * d], F32), sb("o_mem", [P, TPG * d], F32)
        y_rows = [y_mem[:, i * d:(i + 1) * d] for i in range(TPG)]
        o_rows = [o_mem[:, i * d:(i + 1) * d] for i in range(TPG)]
        bn_parts = [sb(f"bn_parts{i}", [P, 6], F32) for i in range(TPG)]
        mean_var = [sb(f"mean_var{i}", [P, 2], F32) for i in range(TPG)]
        std = [sb(f"std{i}", [P, 1], F32) for i in range(TPG)]
        rstd = [sb(f"rstd{i}", [P, 1], F32) for i in range(TPG)]
        neg_mean = [sb(f"neg_mean{i}", [P, 1], F32) for i in range(TPG)]
        eps_col = sb("eps_col", [P, 1], F32)
        base_of = sb("base_of", [P, n_tiles], F32)
        iota_i = sb("iota_i", [P, n_tiles], I32)
        iota_f = sb("iota_f", [P, P], F32)
        iota_p_i, iota_p = sb("iota_p_i", [P, 1], I32), sb("iota_p", [P, 1], F32)
        ident = sb("ident", [P, P], F32)
        below = sb("below", [P, P], F32)
        ones = sb("ones", [P, P], F32)
        n_bounds = TPG + 1
        dst_i, src_i = sb("dst_i", [er, ec], I32), sb("src_i", [er, ec], I32)
        dst_next = sb("dst_next", [er, ec], I32)
        drops = sb("drops", [er, ec], F32)
        drops_sum = sb("drops_sum", [er, 1], F32)
        unsorted_i = sb("unsorted_i", [1, 1], I32)
        pair_rows = sb("pair_rows", [er, ec, 2], U32)
        pad_rows = sb("pad_rows", [P, pad_edges // P, 2], U32)
        row_first = sb("row_first", [er, 2], U32)
        first_diag = sb("first_diag", [er, er], F32)
        bound_i, bound = sb("bound_i", [P, n_bounds], I32), sb("bound", [P, n_bounds], F32)
        last_shift = sb("last_shift", [P, 1], F32)
        rows_below = o_mem[:, 0:n_bounds * er].rearrange("p (c r) -> p c r", r=er)
        row_no, row_no_i = sb("row_no", [P, n_bounds], F32), sb("row_no_i", [P, n_bounds], U32)
        cut_row = [xb_mem[:, 2 * ec * c:2 * ec * (c + 1)].bitcast(U32) for c in range(n_bounds)]
        edges_below = y_mem[:, 0:n_bounds * ec].rearrange("p (c r) -> p c r", r=ec)
        edges_no = sb("edges_no", [P, n_bounds], F32)
        tile_edges, over_half = sb("tile_edges", [P, TPG], F32), sb("over_half", [P, TPG], F32)
        sort_w, sort_parts = 5 * ec, er // 5
        own_no, own_dst2 = sb("own_no", [er, ec], F32), sb("own_dst2", [er, ec], F32)
        place, place_part = sb("place", [er, ec], F32), sb("place_part", [er, 1], F32)
        other_i, other_dst2, is_before, goes_before = (xb_mem[0:er, n * sort_w:(n + 1) * sort_w] for n in range(4))
        other_i = other_i.bitcast(I32)
        local_no, local_no_i = y_mem[0:er, 0:sort_w], y_mem[0:er, sort_w:2 * sort_w].bitcast(I32)
        own_no_i = sb("own_no_i", [er, ec], I32)
        pair_col, place_col = sb("pair_col", [er, 2], U32), sb("place_col", [er, 1], U32)
        extra, extra_i = sb("extra", [P, TPG], F32), sb("extra_i", [P, TPG], I32)
        full_i = sb("full_i", [P, TPG], I32)
        steps_i = sb("steps_i", [P, TPG], I32)
        steps_before = sb("steps_before", [P, TPG + 2], F32)
        tile_info = sb("tile_info", [P, TPG, fields], I32)
        tile_row = sb("tile_row", [1, P * TPG * fields], I32)

        banks = [ctx.enter_context(nc.psum_tensor(f"bank{i}", [P, d], F32)) for i in range(8)]
        agg_ps, ht_ps, l1_ps, l2_ps = banks[0:2], banks[2:4], banks[4:6], banks[6:8]

        w_in = sems("w_in", 2)
        consts_in = sem("consts_in")
        eps_set = sem("eps_set")
        w_hi_done, w_lo_done = sem("w_hi_done"), sem("w_lo_done")
        iotas_done = sem("iotas_done")
        step_dve = sem("step_dve")
        edges_loaded = sem("edges_loaded")
        next_cleared, next_loaded = sem("next_cleared"), sem("next_loaded")
        pairs_made, pairs_stored = sem("pairs_made"), sem("pairs_stored")
        drops_done, drops_counted = sem("drops_done"), sem("drops_counted")
        flag_made = sem("flag_made")
        order_final = sem("order_final")
        firsts_in, diag_made, firsts_spread = sem("firsts_in"), sem("diag_made"), sem("firsts_spread")
        rows_known, cut_rows_in = sem("rows_known"), sems("cut_rows_in", n_bounds)
        totals_made, totals_spread = sem("totals_made"), sem("totals_spread")
        info_made, table_in = sem("info_made"), sem("table_in")
        x_in = [sems(f"x_in{a}", TPG) for a in range(2)]
        edges_in_done = sems("edges_in_done", TPG)
        nbr_in = sems("nbr_in", TPG)
        nbr_hi_done, onehot_done = sem("nbr_hi_done"), sem("onehot_done")
        lo_last_done, lo_first_done = sem("lo_last_done"), sem("lo_first_done")
        agg_done, h_done, ht_done = sem("agg_done"), sem("h_done"), sem("ht_done")
        ht_hi_done, ht_lo_done = sem("ht_hi_done"), sem("ht_lo_done")
        l1_done, relu_done = sem("l1_done"), sem("relu_done")
        r_hi_done, r_lo_done = sem("r_hi_done"), sem("r_lo_done")
        l2_done, xb_done, y_done = sem("l2_done"), sem("xb_done"), sem("y_done")
        bn_done, stats_done, std_done = sem("bn_done"), sem("stats_done"), sem("std_done")
        rstd_done, neg_mean_done = sem("rstd_done"), sem("neg_mean_done")
        norm_done = sem("norm_done")
        stored = sems("stored", TPG)
        more_edges_in = sems("more_edges_in", 2)
        more_src_done = [sems(f"more_src_done{s}", 2) for s in range(2)]
        more_rel_done = [sems(f"more_rel_done{s}", 2) for s in range(2)]
        more_base_done = sem("more_base_done")
        more_nbr_in = [sems(f"more_nbr_in{s}", 2) for s in range(2)]
        more_onehot_done = [sems(f"more_onehot_done{s}", 2) for s in range(2)]
        more_used = [sems(f"more_used{s}", 2) for s in range(2)]
        sort_step = sem("sort_step")
        sort_part_used, sort_part_in = sem("sort_part_used"), sem("sort_part_in")
        sort_column, sort_put = sem("sort_column"), sem("sort_put")

        base_of_made = 2

        block = ctx.enter_context(nc.Block())

        def plus(group, c):
            return group[0], group[1] + c

        def number(group):
            return 2 * group[0] + group[1]

        def visits(group):
            return group[0] + group[1] // 2 + 1

        def tile_of(group, i):
            return plus(group, i // TPG), i % TPG

        def looped(group):
            return not isinstance(group[0], int)

        def is_last(group):
            return not looped(group) and group[1] == last

        def exists(tile):
            group, i = tile
            return looped(group) or 0 <= group[1] < last or (group[1] == last and i < last_tiles)

        def group_exists(group):
            return looped(group) or 0 <= group[1] <= last

        def tile_no(tile):
            group, i = tile
            return 2 * TPG * group[0] + TPG * group[1] + i

        def count(tile):
            return tile_no(tile) + 1

        def width(group):
            return last_tiles * P if is_last(group) else gw

        def rows_of(tile):
            group, i = tile
            if is_last(group):
                return bass.ds(last_base + i * P, P)
            return bass.ds(gw * (last - 1 - group[1]) + i * P - 2 * gw * group[0], P)

        def wait(eng, semaphore, value):
            if isinstance(value, int) and value <= 0:
                return
            eng.wait_ge(semaphore, value)

        def wait_apart(eng, *waits):
            for _, value in waits:
                eng.compute_val(value)
            eng.wait_ge(flag_made, 1)
            for semaphore, value in waits:
                wait(eng, semaphore, value)

        def over_groups(eng, body):
            for c in range(-1, first_looped):
                body((0, c))
            with eng.Fori(0, n_pairs) as m:
                body((m, first_looped))
                body((m, first_looped + 1))
            for c in range(after_loop, last + 2):
                body((0, c))

        def first_of(eng, tile):
            return eng.value_load(tile_row[0:1, bass.ds(fields * tile_no(tile), 1)], min_val=0, max_val=n_edges)

        def kind_of(eng, tile):
            return eng.value_load(tile_row[0:1, bass.ds(fields * tile_no(tile) + 1, 1)], min_val=0, max_val=max_steps + 1)

        def before_of(eng, tile):
            return eng.value_load(tile_row[0:1, bass.ds(fields * tile_no(tile) + 2, 1)], min_val=1,
                                  max_val=max_steps + n_tiles)

        def full_steps_of(eng, tile):
            return eng.value_load(tile_row[0:1, bass.ds(fields * tile_no(tile) + 4, 1)], min_val=0, max_val=max_steps)

        def second_half_of(eng, tile):
            return eng.value_load(tile_row[0:1, bass.ds(fields * tile_no(tile) + 3, 1)], min_val=0,
                                  max_val=n_edges + half_p)

        def load_edges(eng, tile):
            i = tile[1]
            first, second = first_of(eng, tile), second_half_of(eng, tile)
            wait_apart(eng, (onehot_done, count(tile) - TPG), (nbr_in[i], 16 * number(tile[0])))
            eng.dma_start(edges_in[i][0:half_p, :], edge_pairs[bass.ds(first, half_p), :]
                         ).then_inc(edges_in_done[i], 16)
            eng.dma_start(edges_in[i][half_p:P, :], edge_pairs[bass.ds(second, half_p), :]
                         ).then_inc(edges_in_done[i], 16)

        @block.sync
        def _(sp):
            sp.dma_start(dst_i[:], dst.rearrange("(r c) -> r c", c=ec)).then_inc(edges_loaded, 16)
            sp.dma_start(src_i[:], src.rearrange("(r c) -> r c", c=ec)).then_inc(edges_loaded, 16)
            sp.wait_ge(next_cleared, 1)
            sp.dma_start(dst_next[0:er - 1, :], dst[1:1 + (er - 1) * ec].rearrange("(r c) -> r c", c=ec)
                         ).then_inc(next_loaded, 16)
            sp.dma_start(dst_next[er - 1:er, 0:ec - 1], dst[(er - 1) * ec + 1:n_edges].rearrange("(r c) -> r c", r=1)
                         ).then_inc(next_loaded, 16)
            sp.wait_ge(pairs_made, 1)
            sp.dma_start(edge_pairs[0:n_edges, :].rearrange("(r c) t -> r c t", c=ec), pair_rows[:]
                         ).then_inc(pairs_stored, 16)
            sp.dma_start(edge_pairs[n_edges:n_edges + pad_edges, :].rearrange("(r c) t -> r c t", r=P), pad_rows[:]
                         ).then_inc(pairs_stored, 16)
            sp.wait_ge(order_final, 1)
            sp.dma_start(row_first[:], edge_pairs[0:n_edges, :].rearrange("(r c) t -> r c t", c=ec)[:, 0, :]
                         ).then_inc(firsts_in, 16)
            for i in range(TPG):
                sp.dma_start(x_rows[0][i][:], x[rows_of(((0, 0), i)), :]).then_inc(x_in[0][i], 16)
            sp.wait_ge(info_made, 1)
            sp.dma_start(tile_row[:].rearrange("o (p c) -> o p c", p=P), tile_info[:].rearrange("p t c -> p (t c)")
                         ).then_inc(table_in, 16)
            sp.wait_ge(table_in, 16)

            def load_further_edges(tile):
                kind, s = kind_of(sp, tile), tile[1] % 2
                with sp.If(kind > 1):
                    first, before = first_of(sp, tile), before_of(sp, tile)
                    with sp.Fori(0, kind - 1) as k:
                        wait_apart(sp, *[(more_src_done[s][a], before + k) for a in range(2)],
                                   *[(more_rel_done[s][a], before + k) for a in range(2)])
                        sp.dma_start(more_in[s][:], edge_pairs[bass.ds(first + step_edges * k + P, step_edges), :]
                                     .rearrange("(a p) t -> p a t", p=P)).then_inc(more_edges_in[s], 16)
                    sp.nop()

            for i in range(0, TPG, 2):
                load_edges(sp, ((0, 0), i))
            for i in range(3):
                load_further_edges(((0, 0), i))

            def group_loads(group):
                for i in range(TPG):
                    ahead = tile_of(plus(group, 2), i)
                    if exists(ahead):
                        load_edges(sp, ahead)
                    tile = tile_of(plus(group, 1), i + 3)
                    if exists(tile):
                        load_further_edges(tile)
                    if exists(ahead):
                        a = ahead[0][1] % 2
                        wait_apart(sp, (xb_done, count(tile_of(group, i))))
                        sp.dma_start(x_rows[a][i][:], x[rows_of(ahead), :]).then_inc(x_in[a][i], 16)

            over_groups(sp, group_loads)

        @block.gpsimd
        def _(pool):
            nc.gpsimd.iota(iota_i[:, 0:last * TPG], pattern=[[-gw, last], [P, TPG]], base=(last - 1) * gw,
                           channel_multiplier=0).then_inc(iotas_done, 1)
            nc.gpsimd.iota(iota_i[:, last * TPG:], pattern=[[P, last_tiles]], base=last_base,
                           channel_multiplier=0).then_inc(iotas_done, 1)
            nc.gpsimd.iota(iota_p_i[:], pattern=[[0, 1]], base=0, channel_multiplier=1).then_inc(iotas_done, 1)
            nc.gpsimd.iota(bound_i[:], pattern=[[P, n_bounds]], base=(last - 1) * gw, channel_multiplier=-gw
                           ).then_inc(iotas_done, 1)
            nc.gpsimd.iota(iota_f[:], pattern=[[1, P]], base=0, channel_multiplier=0,
                           allow_small_or_imprecise_dtypes=True).then_inc(iotas_done, 1)

            def put_sorted():
                with pool.Fori(0, sort_parts) as q:
                    wait_apart(pool, (sort_part_used, q + 1))
                    pool.dma_start(other_i, dst[bass.ds(q * sort_w, sort_w)].rearrange("(o c) -> o c", o=1)
                                   .to_broadcast([er, sort_w])).then_inc(sort_part_in, 16)
                pool.wait_ge(sort_part_used, sort_parts + 1)
                with pool.Fori(0, ec) as j:
                    nc.gpsimd.tensor_copy(pair_col[:], pair_rows[:, bass.ds(j, 1), :].rearrange("p o t -> p (o t)"))
                    nc.gpsimd.tensor_copy(place_col[:], place[:, bass.ds(j, 1)]).then_inc(sort_column, 1)
                    wait_apart(pool, (sort_column, j + 1))
                    pool.indirect_dma_start(edge_pairs, bass.IndirectOffsetOnAxis(ap=place_col[:], axis=0),
                                            pair_col[:], None).then_inc(sort_put, 16)
                    pool.wait_ge(sort_put, 16 * (j + 1))

            nc.gpsimd.iota(own_no_i[:], pattern=[[1, ec]], base=0, channel_multiplier=ec).then_inc(iotas_done, 1)
            nc.gpsimd.iota(local_no_i, pattern=[[1, sort_w]], base=0, channel_multiplier=0).then_inc(iotas_done, 1)
            for s in range(2):
                for a in range(2):
                    nc.gpsimd.memset(more_src[s][a][:], 0).then_inc(more_src_done[s][a], 1)
                    pool.dma_start(more_start[:, 2 * s + a, :], x[0:P, 0:4]).then_inc(more_nbr_in[s][a], 16)
                    nc.gpsimd.memset(more_onehot[s][a][:], 0.0).then_inc(more_onehot_done[s][a], 1)
                    nc.gpsimd.memset(more_rel[s][a][:], 0.0).then_inc(more_rel_done[s][a], 1)
            pool.wait_ge(flag_made, 1)
            pool.wait_ge(pairs_stored, 32)
            unsorted = pool.value_load(unsorted_i[:], min_val=0, max_val=n_edges)
            with pool.If(unsorted > 0):
                put_sorted()
                pool.nop()
            nc.gpsimd.memset(more_base[0][:], 0.0).then_inc(order_final, 1)
            pool.wait_ge(rows_known, 1)
            edge_rows = edge_pairs[0:n_edges, :].rearrange("(r c) t -> r (c t)", c=ec)
            for c in range(n_bounds):
                pool.indirect_dma_start(cut_row[c], None, edge_rows,
                                        bass.IndirectOffsetOnAxis(ap=row_no_i[:, c:c + 1], axis=0)
                                        ).then_inc(cut_rows_in[c], 16)

            def gather(tile):
                i = tile[1]
                wait_apart(pool, (edges_in_done[i], 32 * (number(tile[0]) + 1)), (nbr_hi_done, count(tile) - TPG),
                           (lo_last_done, count(tile) - TPG), (lo_first_done, count(tile) - TPG))
                pool.indirect_dma_start(nbr[i][:], None, x,
                                        bass.IndirectOffsetOnAxis(ap=edges_in[i][:, 0:1], axis=0)
                                        ).then_inc(nbr_in[i], 16)

            def split_lo_first(tile):
                i = tile[1]
                pool.wait_ge(nbr_hi_done, count(tile))
                wait(pool, agg_done, count(tile) - 2)
                nc.gpsimd.tensor_tensor(lo_hi[i % 2][0:half_p, :], nbr[i][0:half_p, :],
                                        hi_lo[i % 2][0:half_p, :].bitcast(F32), ALU.subtract
                                        ).then_inc(lo_first_done, 1)

            def further_steps(tile):
                kind, s = kind_of(pool, tile), tile[1] % 2
                base = more_base[tile[1]]
                nc.gpsimd.tensor_copy(base[:], base_of[:, bass.ds(tile_no(tile), 1)]).then_inc(more_base_done, 1)
                with pool.If(kind > 1):
                    before = before_of(pool, tile)
                    wait_apart(pool, (more_base_done, count(tile)))
                    with pool.Fori(0, kind - 1) as k:
                        for a in range(2):
                            wait_apart(pool, (more_edges_in[s], 16 * (before + k)), (more_used[s][a], before + k))
                            nc.gpsimd.tensor_copy(more_src[s][a][:], more_in[s][:, a, 0:1]
                                                  ).then_inc(more_src_done[s][a], 1)
                            nc.gpsimd.tensor_tensor(more_rel[s][a][:], more_in[s][:, a, 1:2].bitcast(F32), base[:],
                                                    ALU.subtract).then_inc(more_rel_done[s][a], 1)
                            wait_apart(pool, (more_src_done[s][a], before + k + 1))
                            pool.indirect_dma_start(more_nbr[s][a], None, x,
                                                    bass.IndirectOffsetOnAxis(ap=more_src[s][a][:], axis=0)
                                                    ).then_inc(more_nbr_in[s][a], 16)
                        wait_apart(pool, *[(more_rel_done[s][a], before + k + 1) for a in range(2)])
                        for a in range(2):
                            nc.gpsimd.tensor_scalar(more_onehot[s][a][:], iota_f[:], more_rel[s][a][:], None, ALU.is_equal
                                                    ).then_inc(more_onehot_done[s][a], 1)
                    pool.nop()

            pool.wait_ge(table_in, 16)
            pool.wait_ge(step_dve, base_of_made)
            pool.wait_ge(w_lo_done, 2)
            for i in range(TPG - 1):
                gather(((0, 0), i))
            split_lo_first(((0, 0), 0))
            for i in range(2):
                further_steps(((0, 0), i))

            def group_edges(group):
                for i in range(TPG):
                    for tile, work in ((tile_of(plus(group, 1), i + 3), gather),
                                       (tile_of(plus(group, 1), i + 1), split_lo_first),
                                       (tile_of(plus(group, 1), i + 2), further_steps)):
                        if exists(tile):
                            work(tile)

            over_groups(pool, group_edges)

        @block.scalar
        def _(act):
            act.wait_ge(next_loaded, 32)
            act.wait_ge(pairs_stored, 32)
            act.dma_start(w_stage[:], w1.rearrange("(k p) n -> p k n", p=P)).then_inc(w_in[0], 16)
            act.dma_start(b1_col[:], b1.rearrange("(k p) -> p k", p=P),
                          allow_slow_non_contiguous=True).then_inc(consts_in, 16)
            act.dma_start(b2_rows[:], b2.rearrange("(o n) -> o n", o=1).to_broadcast([P, d])
                          ).then_inc(consts_in, 16)
            for n, (hi, w) in enumerate(((w1_hi, w2), (w2_hi, None))):
                act.wait_ge(w_in[n], 16)
                nc.scalar.copy(hi[:], w_stage[:]).then_inc(w_hi_done, 1)
                if w is not None:
                    act.wait_ge(w_lo_done, 1)
                    act.dma_start(w_stage[:], w.rearrange("(k p) n -> p k n", p=P)).then_inc(w_in[1], 16)
            act.wait_ge(consts_in, 32)
            act.wait_ge(eps_set, 1)

            def split_hi(tile):
                i = tile[1]
                act.wait_ge(nbr_in[i], 16 * (number(tile[0]) + 1))
                wait(act, agg_done, count(tile) - 2)
                nc.scalar.copy(hi_lo[i % 2][0:half_p, :], nbr[i][0:half_p, :])
                nc.scalar.copy(lo_hi[i % 2][half_p:P, :], nbr[i][half_p:P, :]).then_inc(nbr_hi_done, 1)

            act.wait_ge(table_in, 16)
            for i in range(1, TPG, 2):
                load_edges(act, ((0, 0), i))
            split_hi(((0, 0), 0))

            def group_act(group):
                for i in range(TPG):
                    half = group[1] % 2
                    n = width(group) if group_exists(group) else 0
                    block_no = count((group, i))
                    tile = tile_of(plus(group, 1), i + 1)
                    if exists(tile):
                        split_hi(tile)
                    if group_exists(group):
                        act.wait_ge(l1_done, block_no)
                        wait(act, r_lo_done, block_no - 2)
                        nc.scalar.activation(relu_f[i % 2][:, 0:n], l1_ps[i % 2][:, 0:n], ACT.Relu,
                                             bias=b1_col[:, i:i + 1]).then_inc(relu_done, 1)
                    tile = tile_of(plus(group, 1), i)
                    if exists(tile):
                        act.wait_ge(ht_done, count(tile))
                        nc.scalar.copy(ht_hi[1 - half][:, :, i * P:(i + 1) * P],
                                       ht_ps[i % 2][:].rearrange("p (k n) -> p k n", n=P)).then_inc(ht_hi_done, 1)
                    if group_exists(group):
                        act.wait_ge(relu_done, block_no)
                        wait(act, l2_done, count((plus(group, -2), TPG - 1)))
                        nc.scalar.copy(r_hi[half][:, i, 0:n], relu_f[i % 2][:, 0:n]).then_inc(r_hi_done, 1)
                    tile = tile_of(plus(group, -1), i - 2)
                    if exists(tile):
                        normalise(tile)
                    tile = tile_of(plus(group, -1), i - 1)
                    if exists(tile):
                        act.wait_ge(stats_done, count(tile))
                        nc.scalar.activation(std[tile[1]][:], mean_var[tile[1]][:, 1:2], ACT.Sqrt,
                                             bias=eps_col[:]).then_inc(std_done, 1)

            def normalise(tile):
                group, i = tile
                act.wait_ge(neg_mean_done, count(tile))
                wait(act, stored[i], 16 * number(group))
                nc.scalar.activation(o_rows[i], y_rows[i], ACT.Identity, bias=neg_mean[i][:],
                                     scale=rstd[i][:]).then_inc(norm_done, 1)
                act.wait_ge(norm_done, count(tile))
                if is_last(group) and i == 0:
                    if last_skip < P:
                        act.dma_start(out[last * gw:last_base + P, :], o_rows[i][last_skip:P, :]
                                      ).then_inc(stored[i], 16)
                else:
                    act.dma_start(out[rows_of(tile), :], o_rows[i]).then_inc(stored[i], 16)

            over_groups(act, group_act)
            for tile in (tile_of((0, last + 1), i - 2) for i in range(TPG)):
                if exists(tile):
                    normalise(tile)
            for i in range(TPG):
                act.wait_ge(stored[i], 16 * (last + (1 if i < last_tiles else 0)))

        @block.vector
        def _(dve):
            chain = [0]

            def then(instruction):
                chain[0] += 1
                instruction.then_inc(step_dve, 1)
                dve.wait_ge(step_dve, chain[0])

            V = nc.vector
            V.memset(dst_next[:], 1 << 24).then_inc(next_cleared, 1)
            V.memset(eps_col[:], EPS).then_inc(eps_set, 1)
            V.memset(pad_rows[:, :, 0], 0)
            V.memset(pad_rows[:, :, 1].bitcast(F32), -1.0)
            then(V.memset(ones[:], 1.0))
            dve.wait_ge(iotas_done, 5)
            V.tensor_copy(bound[:], bound_i[:])
            V.tensor_copy(base_of[:], iota_i[:])
            then(V.tensor_copy(iota_p[:], iota_p_i[:]))
            V.tensor_scalar(ident[:], iota_f[:], iota_p[:], None, ALU.is_equal)
            V.tensor_scalar(below[:], iota_f[:], iota_p[:], None, ALU.is_gt)
            then(V.tensor_scalar(last_shift[:], iota_p[:], float(last), float(last_base + gw), ALU.is_equal, ALU.mult))
            then(V.tensor_scalar(bound[:], bound[:], last_shift[:], None, ALU.add))

            dve.wait_ge(edges_loaded, 32)
            V.tensor_copy(pair_rows[:, :, 0], src_i[:])
            V.tensor_copy(pair_rows[:, :, 1].bitcast(F32), dst_i[:]).then_inc(pairs_made, 1)
            dve.wait_ge(next_loaded, 32)
            then(V.tensor_tensor(drops[:], dst_next[:], dst_i[:], ALU.is_lt))
            V.tensor_reduce(drops_sum[:], drops[:], AX_X, ALU.add).then_inc(drops_done, 1)
            dve.wait_ge(drops_counted, 1)
            V.tensor_copy(unsorted_i[:], banks[0][0:1, 0:1]).then_inc(flag_made, 1)

            def split_weights(n, hi, lo):
                dve.wait_ge(w_hi_done, n + 1)
                V.tensor_tensor(lo[:], w_stage[:], hi[:].bitcast(F32), ALU.subtract).then_inc(w_lo_done, 1)


            def find_places():
                per_column, per_part = 4, 2

                def step(instruction, value):
                    instruction.then_inc(sort_step, 1)
                    dve.wait_ge(sort_step, value)

                V.tensor_copy(own_no[:], own_no_i[:])
                V.tensor_copy(local_no, local_no_i)
                V.memset(place[:], 0.0)
                step(V.tensor_scalar(own_dst2[:], dst_i[:], 2.0, None, ALU.mult), 1)
                V.memset(place_part[:], 0.0).then_inc(sort_part_used, 1)
                with dve.Fori(0, sort_parts) as q:
                    at_part = 1 + q * (per_part + per_column * ec)
                    dve.wait_ge(sort_part_in, 16 * (q + 1))
                    V.tensor_scalar(other_dst2, other_i, 2.0, None, ALU.mult).then_inc(sort_step, 1)
                    wait_apart(dve, (sort_step, at_part + 1))
                    with dve.Fori(0, ec) as j:
                        at = at_part + 1 + per_column * j
                        step(V.tensor_scalar(is_before, local_no, own_no[:, bass.ds(j, 1)], None, ALU.is_lt),
                             at + 1)
                        step(V.scalar_tensor_tensor(out=goes_before, in0=other_dst2,
                                                    scalar=own_dst2[:, bass.ds(j, 1)], in1=is_before,
                                                    op0=ALU.subtract, op1=ALU.is_lt), at + 2)
                        step(V.tensor_reduce(place_part[:], goes_before, AX_X, ALU.add), at + 3)
                        step(V.tensor_tensor(place[:, bass.ds(j, 1)], place[:, bass.ds(j, 1)], place_part[:],
                                             ALU.add), at + 4)
                    step(V.tensor_scalar(own_no[:], own_no[:], float(sort_w), None, ALU.subtract),
                         at_part + 2 + per_column * ec)
                    V.memset(place_part[:], 0.0).then_inc(sort_part_used, 1)

            dve.wait_ge(flag_made, 1)
            unsorted = dve.value_load(unsorted_i[:], min_val=0, max_val=n_edges)
            with dve.If(unsorted > 0):
                dve.wait_ge(iotas_done, 7)
                find_places()
                dve.nop()

            dve.wait_ge(firsts_in, 16)
            V.tensor_scalar(first_diag[:], ident[0:er, 0:er], row_first[:, 1:2].bitcast(F32), None, ALU.mult
                            ).then_inc(diag_made, 1)
            dve.wait_ge(firsts_spread, 1)
            for c in range(n_bounds):
                ins = V.tensor_scalar(rows_below[:, c, :], banks[1][:, 0:er], bound[:, c:c + 1], None, ALU.is_lt)
            then(ins)
            then(V.tensor_reduce(row_no[:], rows_below, AX_X, ALU.add))
            then(V.tensor_scalar(row_no[:], row_no[:], 1.0, 0.0, ALU.subtract, ALU.max))
            V.tensor_copy(row_no_i[:], row_no[:]).then_inc(rows_known, 1)
            split_weights(0, w1_hi, w1_lo)
            for c in range(n_bounds):
                dve.wait_ge(cut_rows_in[c], 16)
                ins = V.tensor_scalar(edges_below[:, c, :],
                                      cut_row[c].rearrange("p (c t) -> p c t", t=2)[:, :, 1].bitcast(F32),
                                      bound[:, c:c + 1], None, ALU.is_lt)
            then(ins)
            then(V.tensor_reduce(edges_no[:], edges_below, AX_X, ALU.add))
            then(V.scalar_tensor_tensor(out=edges_no[:], in0=row_no[:], scalar=float(ec), in1=edges_no[:],
                                        op0=ALU.mult, op1=ALU.add))
            then(V.tensor_tensor(tile_edges[:], edges_no[:, 1:n_bounds], edges_no[:, 0:TPG], ALU.subtract))
            V.tensor_scalar(over_half[:], tile_edges[:], float(half_p), None, ALU.is_gt)
            then(V.tensor_scalar(extra[:], tile_edges[:], float(P), 0.0, ALU.subtract, ALU.max))
            V.tensor_scalar(full_i[:], extra[:], float(P - 1), None, ALU.add)
            then(V.tensor_scalar(extra_i[:], extra[:], float(step_edges - 1), None, ALU.add))
            V.tensor_scalar(tile_info[:, :, 4], full_i[:], step_bits, None, ALU.logical_shift_right)
            then(V.tensor_scalar(steps_i[:], extra_i[:], step_bits, None, ALU.logical_shift_right))
            V.tensor_copy(extra[:], steps_i[:])
            then(V.memset(steps_before[:, 0:2], 0.0))
            for i in range(0, TPG, 2):
                then(V.tensor_tensor(steps_before[:, i + 2:i + 4], steps_before[:, i:i + 2], extra[:, i:i + 2],
                                     ALU.add))
            V.tensor_tensor(tile_info[:, :, 1], extra[:], over_half[:], ALU.add).then_inc(totals_made, 1)
            V.scalar_tensor_tensor(out=tile_info[:, :, 3], in0=over_half[:], scalar=float(half_p),
                                   in1=edges_no[:, 0:TPG], op0=ALU.mult, op1=ALU.add)
            dve.wait_ge(totals_spread, 1)
            V.tensor_copy(tile_info[:, :, 0], edges_no[:, 0:TPG])
            for s in range(2):
                ins = V.tensor_scalar(tile_info[:, s:TPG:2, 2], steps_before[:, s:TPG:2], banks[0][:, 4 + s:5 + s],
                                      1.0, ALU.add, ALU.add)
            ins.then_inc(info_made, 1)

            def one_hot(tile):
                group, i = tile
                dve.wait_ge(edges_in_done[i], 32 * (number(group) + 1))
                wait(dve, agg_done, count(tile) - 2)
                V.tensor_scalar(onehot[i % 2][:], iota_f[:],
                                base_of[:, bass.ds(tile_no(tile), 1)],
                                edges_in[i][:, 1:2].bitcast(F32), ALU.add, ALU.is_equal).then_inc(onehot_done, 1)

            def split_lo_last(tile):
                i = tile[1]
                dve.wait_ge(nbr_hi_done, count(tile))
                V.tensor_tensor(hi_lo[i % 2][half_p:P, :], nbr[i][half_p:P, :],
                                lo_hi[i % 2][half_p:P, :].bitcast(F32), ALU.subtract).then_inc(lo_last_done, 1)

            split_weights(1, w2_hi, w2_lo)
            dve.wait_ge(consts_in, 32)
            one_hot(((0, 0), 0))
            split_lo_last(((0, 0), 0))

            def group_dve(group):
                half = group[1] % 2
                for i in range(TPG):
                    tile = tile_of(plus(group, 1), i)
                    if exists(tile):
                        dve.wait_ge(agg_done, count(tile))
                        dve.wait_ge(x_in[1 - half][i], 16 * visits(plus(group, 1)))
                        wait(dve, ht_done, count(tile) - 2)
                        V.tensor_tensor(h_rows[i % 2][:], agg_ps[i % 2][:], x_rows[1 - half][i][:], ALU.add
                                        ).then_inc(h_done, 1)
                    tile = tile_of(plus(group, 1), i + 1)
                    if exists(tile):
                        one_hot(tile)
                        split_lo_last(tile)
                    tile = tile_of(plus(group, -1), i - 1)
                    if exists(tile):
                        residual(tile)
                    tile = tile_of(group, i)
                    if exists(tile):
                        dve.wait_ge(h_done, count(tile))
                        wait(dve, y_done, count(tile) - 2 * TPG)
                        V.tensor_tensor(xb_rows[half][i], x_rows[half][i][:], b2_rows[:], ALU.add
                                        ).then_inc(xb_done, 1)
                    tile = tile_of(plus(group, 1), i)
                    if exists(tile):
                        dve.wait_ge(ht_hi_done, count(tile))
                        V.tensor_tensor(ht_lo[1 - half][:, :, i * P:(i + 1) * P],
                                        ht_ps[i % 2][:].rearrange("p (k n) -> p k n", n=P),
                                        ht_hi[1 - half][:, :, i * P:(i + 1) * P].bitcast(F32), ALU.subtract
                                        ).then_inc(ht_lo_done, 1)
                    if group_exists(group):
                        n = width(group)
                        dve.wait_ge(r_hi_done, count((group, i)))
                        V.tensor_tensor(r_lo[half][:, i, 0:n], relu_f[i % 2][:, 0:n],
                                        r_hi[half][:, i, 0:n].bitcast(F32), ALU.subtract).then_inc(r_lo_done, 1)
                    tile = tile_of(plus(group, -1), i - 1)
                    if exists(tile):
                        scale_of(tile)

            def residual(tile):
                group, i = tile
                dve.wait_ge(l2_done, count(tile))
                dve.wait_ge(xb_done, count(tile))
                wait(dve, norm_done, count(tile) - TPG)
                V.tensor_tensor(y_rows[i], l2_ps[i % 2][:], xb_rows[group[1] % 2][i], ALU.add
                                ).then_inc(y_done, 1)
                dve.wait_ge(y_done, count(tile))
                V.bn_stats(bn_parts[i][:], y_rows[i]).then_inc(bn_done, 1)
                wait_apart(dve, (bn_done, count(tile)))
                V.bn_aggr(mean_var[i][:], bn_parts[i][:]).then_inc(stats_done, 1)

            def scale_of(tile):
                _, i = tile
                dve.wait_ge(std_done, count(tile))
                V.reciprocal(rstd[i][:], std[i][:]).then_inc(rstd_done, 1)
                dve.wait_ge(rstd_done, count(tile))
                V.tensor_scalar(neg_mean[i][:], mean_var[i][:, 0:1], rstd[i][:], -1.0, ALU.mult, ALU.mult
                                ).then_inc(neg_mean_done, 1)

            over_groups(dve, group_dve)

        @block.tensor
        def _(pe):
            pe.wait_ge(step_dve, 1)
            pe.wait_ge(drops_done, 1)
            nc.tensor.matmul(banks[0][0:1, 0:1], drops_sum[:], ones[0:er, 0:1], start=True, stop=True
                             ).then_inc(drops_counted, 1)
            for s in range(2):
                for a in range(2):
                    nc.tensor.matmul(banks[2 + 2 * s + a][:, 0:1], ones[:], ones[:, 0:1], start=True, stop=True
                                     ).then_inc(more_used[s][a], 1)
            pe.wait_ge(diag_made, 1)
            nc.tensor.matmul(banks[1][:, 0:er], ones[0:er, :], first_diag[:], start=True, stop=True
                             ).then_inc(firsts_spread, 1)
            pe.wait_ge(totals_made, 1)
            nc.tensor.matmul(banks[0][:, 4:6], below[:], steps_before[:, TPG:TPG + 2], start=True, stop=True
                             ).then_inc(totals_spread, 1)
            pe.wait_ge(info_made, 1)
            pe.wait_ge(w_lo_done, 2)
            pe.wait_ge(table_in, 16)

            def more_product(s, a, steps, n):
                bank = agg_ps[s]
                pe.wait_ge(more_nbr_in[s][a], 16 * (steps + 1))
                pe.wait_ge(more_onehot_done[s][a], steps + 1)
                nc.tensor.matmul(bank[:, 0:n], more_onehot[s][a][:], more_nbr[s][a][:, 0:n], start=False, stop=False
                                 ).then_inc(more_used[s][a], 1)

            def aggregate(tile):
                kind = kind_of(pe, tile)
                i, s = tile[1], tile[1] % 2
                bank = agg_ps[i % 2]
                nodes, first, second = onehot[i % 2], hi_lo[i % 2], lo_hi[i % 2]
                pe.wait_ge(onehot_done, count(tile))
                pe.wait_ge(lo_last_done, count(tile))
                wait(pe, h_done, count(tile) - 2)
                with pe.If(kind > 0):
                    nc.tensor.matmul(bank[:], nodes[:], first[:], start=True, stop=False)
                    with pe.If(kind > 1):
                        before, full = before_of(pe, tile), full_steps_of(pe, tile)
                        with pe.If(full > 0):
                            with pe.Fori(0, full) as k:
                                for a in range(2):
                                    more_product(s, a, before + k, d)
                            pe.nop()
                        with pe.If(kind - full > 1):
                            more_product(s, 0, before + full, d)
                            more_product(s, 1, before + full, 1)
                            pe.nop()
                        pe.nop()
                    pe.wait_ge(lo_first_done, count(tile))
                    nc.tensor.matmul(bank[:], nodes[:], second[:], start=False, stop=True).then_inc(agg_done, 1)
                with pe.Else():
                    pe.wait_ge(lo_first_done, count(tile))
                    nc.tensor.matmul(bank[:], nodes[:], first[:], start=True, stop=True).then_inc(agg_done, 1)

            def transpose(tile):
                i = tile[1]
                pe.wait_ge(h_done, count(tile))
                wait(pe, ht_lo_done, count(tile) - 2)
                for k in range(kb_n):
                    ins = nc.tensor.transpose(ht_ps[i % 2][:, k * P:(k + 1) * P], h_rows[i % 2][:, k * P:(k + 1) * P],
                                              ident[:])
                ins.then_inc(ht_done, 1)

            def layer1(group, f):
                half, n = group[1] % 2, width(group)
                tiles = last_tiles if is_last(group) else TPG
                pe.wait_ge(ht_lo_done, count((group, tiles - 1)))
                wait(pe, relu_done, count((group, f)) - 2)
                terms = [(w1_hi, ht_hi[half]), (w1_hi, ht_lo[half]), (w1_lo, ht_hi[half])]
                for k in range(kb_n):
                    for t, (w, h) in enumerate(terms):
                        ins = nc.tensor.matmul(l1_ps[f % 2][:, 0:n], w[:, k, f * P:(f + 1) * P], h[:, k, 0:n],
                                               start=(t == 0 and k == 0), stop=(t == 2 and k == kb_n - 1))
                ins.then_inc(l1_done, 1)

            def layer2(tile):
                group, i = tile
                half = group[1] % 2
                pe.wait_ge(r_lo_done, count((group, TPG - 1)))
                wait(pe, y_done, count(tile) - 2)
                terms = [(r_hi[half], w2_hi), (r_hi[half], w2_lo), (r_lo[half], w2_hi)]
                for k in range(kb_n):
                    for t, (r, w) in enumerate(terms):
                        ins = nc.tensor.matmul(l2_ps[i % 2][:], r[:, k, i * P:(i + 1) * P], w[:, k, :],
                                               start=(t == 0 and k == 0), stop=(t == 2 and k == kb_n - 1))
                ins.then_inc(l2_done, 1)

            def group_products(group):
                for i in range(TPG):
                    tile = tile_of(plus(group, 1), i)
                    if exists(tile):
                        aggregate(tile)
                    if group_exists(group):
                        layer1(group, i)
                    if exists(tile):
                        transpose(tile)
                    tile = tile_of(plus(group, -1), i)
                    if exists(tile):
                        layer2(tile)

            over_groups(pe, group_products)


_INS = ["x", "src", "dst", "L0_gnn_W1", "L0_gnn_b1", "L0_gnn_W2", "L0_gnn_b2"]


def kernel(**inputs):
    import numpy as _np
    import concourse.bacc as _bacc
    from concourse import mybir as _mybir
    from concourse.bass_utils import run_bass_kernel_spmd as _run

    nc = _bacc.Bacc("TRN2", target_bir_lowering=False, num_devices=1)
    arrays, args = {}, []
    for name in _INS:
        a = _np.ascontiguousarray(inputs[name])
        arrays[f"in_{name}_dram"] = a
        args.append(nc.dram_tensor(f"in_{name}_dram", a.shape, _mybir.dt.from_np(a.dtype), kind="ExternalInput").ap())
    out = nc.dram_tensor("out_dram", inputs["x"].shape, _mybir.dt.float32, kind="ExternalOutput").ap()
    gnn_layer_with_residual_norm(nc, *args, out)
    r = _run(nc, [arrays], core_ids=[0])
    return r.results[0]["out_dram"]
```
